# Optimizing a Trainium2 kernel written in Bass

```python
import numpy as np
import jax
import jax.numpy as jnp

def _softmax(x, axis=-1):
    return jax.nn.softmax(x, axis=axis)

def _gelu(x):
    return jax.nn.gelu(x, approximate=True)

def _silu(x):
    return jax.nn.silu(x)

def _sigmoid(x):
    return jax.nn.sigmoid(x)

def _layernorm(x, axis=-1, eps=1e-05):
    m = jnp.mean(x, axis=axis, keepdims=True)
    v = jnp.var(x, axis=axis, keepdims=True)
    return (x - m) / jnp.sqrt(v + eps)

def _scatter_add(tgt, idx, src, axis=0):
    return tgt.at[idx].add(src)

def _segment_sum(src, seg, n):
    return jax.ops.segment_sum(src, seg, n)
kernel_name = 'mk_flamingo_gated_d1_seqx_r8_ada65b'

def setup_inputs(seed: int=0):
    np.random.seed(seed)
    _w = jnp.asarray

    def _rec_inputs():
        import jax
        import jax.numpy as jnp
        _rk = jax.random.key(seed)
        x = -0.0005207 + 1.001 * jax.random.normal(jax.random.fold_in(_rk, 1), (8, 128, 512), jnp.float32)
        _lenS = 128 - jax.random.randint(jax.random.fold_in(_rk, 7), (8,), 0, max(1, 128 // 4) + 1, jnp.int32)
        _lenS2 = 128 - jax.random.randint(jax.random.fold_in(_rk, 8), (8,), 0, max(1, 128 // 4) + 1, jnp.int32)
        _ctx_4096P = jax.random.normal(jax.random.fold_in(_rk, 11), (8, 16, 512), jnp.float32)
        _ctx_4096c = jax.random.dirichlet(jax.random.fold_in(_rk, 511), 0.3 * jnp.ones((16,), jnp.float32), (8, 128))
        _ctx_4096t = jnp.einsum('bsk,bkd->bsd', _ctx_4096c, _ctx_4096P)
        _ctx_4096t = _ctx_4096t * jax.lax.rsqrt(jnp.mean(jnp.square(_ctx_4096t)) + 1e-12) * 0.953939
        ctx_4096 = -0.00010331 + 0.999899 * (_ctx_4096t + 0.3 * jax.random.normal(jax.random.fold_in(_rk, 611), (8, 128, 512), jnp.float32))
        _g = jax.random.normal(jax.random.fold_in(_rk, 9001), (2, 1), jnp.float32)
        _g = jnp.sign(_g) * jnp.maximum(jnp.abs(_g), 1.0) + (_g == 0) * 1.0
        g_xattn = _g[0]
        g_ffn = _g[1]
        return (x, ctx_4096, g_xattn, g_ffn)
    x, ctx_4096, g_xattn, g_ffn = _rec_inputs()

    def _L0_xattn_setup():
        import jax, jax.numpy as jnp
        import numpy as np
        B, Q, D = (8, 64, 512)
        CTX = 512
        H, KV, HD = (16, 4, 96)
        G = H // KV
        key = jax.random.key(seed)
        ks = jax.random.split(key, 6)
        s = 0.02
        return {'latents': jax.random.normal(ks[0], (B, Q, D), jnp.float32), 'context': jax.random.normal(ks[1], (B, CTX, D), jnp.float32), 'Wq': jax.random.normal(ks[2], (H * HD, D), jnp.float32) * s, 'Wk': jax.random.normal(ks[3], (KV * HD, D), jnp.float32) * s, 'Wv': jax.random.normal(ks[4], (KV * HD, D), jnp.float32) * s, 'Wo': jax.random.normal(ks[5], (D, H * HD), jnp.float32) * s}
    _L0_xattn_all = _L0_xattn_setup()
    _L0_xattn_in = {k: v for k, v in _L0_xattn_all.items() if k in ('Wq', 'Wk', 'Wv', 'Wo')}
    del _L0_xattn_all

    def _L0_ffn_setup():
        import jax, jax.numpy as jnp
        import numpy as np
        HID = 512
        INTER = 1376
        BITS = 4
        PACK = 8
        MAXQ = 15
        GROUP = 128

        def _dequant(qweight, scales, qzeros, g_idx):
            shifts = jnp.arange(PACK, dtype=jnp.uint32) * BITS
            qw = qweight.astype(jnp.uint32)
            w = (qw[:, None, :] >> shifts[None, :, None] & MAXQ).reshape(-1, qweight.shape[1])
            qz = qzeros.astype(jnp.uint32)
            z = ((qz[:, :, None] >> shifts[None, None, :] & MAXQ) + 1).reshape(qzeros.shape[0], -1)
            s = scales[g_idx]
            return (w.astype(scales.dtype) - z[g_idx].astype(scales.dtype)) * s
        key = jax.random.key(seed)
        ks = jax.random.split(key, 16)

        def qw(k, K, N):
            return jax.random.randint(k, (K // PACK, N), 0, 2147483647, dtype=jnp.int32)

        def qz(k, G, N):
            return jax.random.randint(k, (G, N // PACK), 0, 2147483647, dtype=jnp.int32)

        def sc(k, G, N):
            return jax.random.uniform(k, (G, N), jnp.float32, 0.001, 0.01)
        Gk = HID // GROUP
        Gd = INTER // GROUP
        return {'x': jax.random.normal(ks[0], (4, 256, HID), jnp.float32), 'gate_qweight': qw(ks[1], HID, INTER), 'gate_scales': sc(ks[2], Gk, INTER), 'gate_qzeros': qz(ks[3], Gk, INTER), 'gate_g_idx': (jnp.arange(HID) // GROUP).astype(jnp.int32), 'up_qweight': qw(ks[4], HID, INTER), 'up_scales': sc(ks[5], Gk, INTER), 'up_qzeros': qz(ks[6], Gk, INTER), 'up_g_idx': (jnp.arange(HID) // GROUP).astype(jnp.int32), 'down_qweight': qw(ks[7], INTER, HID), 'down_scales': sc(ks[8], Gd, HID), 'down_qzeros': qz(ks[9], Gd, HID), 'down_g_idx': (jnp.arange(INTER) // GROUP).astype(jnp.int32)}
    _L0_ffn_all = _L0_ffn_setup()
    _L0_ffn_in = {k: v for k, v in _L0_ffn_all.items() if k in ('gate_qweight', 'gate_scales', 'gate_qzeros', 'gate_g_idx', 'up_qweight', 'up_scales', 'up_qzeros', 'up_g_idx', 'down_qweight', 'down_scales', 'down_qzeros', 'down_g_idx')}
    del _L0_ffn_all
    return {'x': x, 'ctx_4096': ctx_4096, 'g_xattn': g_xattn, 'g_ffn': g_ffn, 'L0_xattn_Wq': _L0_xattn_in['Wq'], 'L0_xattn_Wk': _L0_xattn_in['Wk'], 'L0_xattn_Wv': _L0_xattn_in['Wv'], 'L0_xattn_Wo': _L0_xattn_in['Wo'], 'L0_ffn_gate_qweight': _L0_ffn_in['gate_qweight'], 'L0_ffn_gate_scales': _L0_ffn_in['gate_scales'], 'L0_ffn_gate_qzeros': _L0_ffn_in['gate_qzeros'], 'L0_ffn_gate_g_idx': _L0_ffn_in['gate_g_idx'], 'L0_ffn_up_qweight': _L0_ffn_in['up_qweight'], 'L0_ffn_up_scales': _L0_ffn_in['up_scales'], 'L0_ffn_up_qzeros': _L0_ffn_in['up_qzeros'], 'L0_ffn_up_g_idx': _L0_ffn_in['up_g_idx'], 'L0_ffn_down_qweight': _L0_ffn_in['down_qweight'], 'L0_ffn_down_scales': _L0_ffn_in['down_scales'], 'L0_ffn_down_qzeros': _L0_ffn_in['down_qzeros'], 'L0_ffn_down_g_idx': _L0_ffn_in['down_g_idx']}

def reference(x, ctx_4096, g_xattn, g_ffn, L0_xattn_Wq, L0_xattn_Wk, L0_xattn_Wv, L0_xattn_Wo, L0_ffn_gate_qweight, L0_ffn_gate_scales, L0_ffn_gate_qzeros, L0_ffn_gate_g_idx, L0_ffn_up_qweight, L0_ffn_up_scales, L0_ffn_up_qzeros, L0_ffn_up_g_idx, L0_ffn_down_qweight, L0_ffn_down_scales, L0_ffn_down_qzeros, L0_ffn_down_g_idx):
    import jax
    import jax.numpy as jnp

    def _L0_xattn_ref(latents, context, Wq, Wk, Wv, Wo):
        import jax, jax.numpy as jnp
        import numpy as np
        B, Q, D = (8, 64, 512)
        CTX = 512
        H, KV, HD = (16, 4, 96)
        G = H // KV
        b, q_len, _ = latents.shape
        hidden = jnp.concatenate([context, latents], axis=1)
        s_len = hidden.shape[1]
        q = (latents @ Wq.T).reshape(b, q_len, H, HD)
        k = (hidden @ Wk.T).reshape(b, s_len, KV, HD)
        v = (hidden @ Wv.T).reshape(b, s_len, KV, HD)
        q = q.transpose(0, 2, 1, 3).reshape(b, KV, G, q_len, HD)
        k = k.transpose(0, 2, 1, 3)
        v = v.transpose(0, 2, 1, 3)
        scale = 1.0 / jnp.sqrt(jnp.asarray(HD, q.dtype))
        scores = jnp.einsum('bkgqd,bksd->bkgqs', q, k) * scale
        attn = jax.nn.softmax(scores.astype(jnp.float32), axis=-1).astype(q.dtype)
        out = jnp.einsum('bkgqs,bksd->bkgqd', attn, v)
        out = out.reshape(b, H, q_len, HD).transpose(0, 2, 1, 3).reshape(b, q_len, H * HD)
        return out @ Wo.T

    def _L0_ffn_ref(x, gate_qweight, gate_scales, gate_qzeros, gate_g_idx, up_qweight, up_scales, up_qzeros, up_g_idx, down_qweight, down_scales, down_qzeros, down_g_idx):
        import jax, jax.numpy as jnp
        import numpy as np
        HID = 512
        INTER = 1376
        BITS = 4
        PACK = 8
        MAXQ = 15
        GROUP = 128

        def _dequant(qweight, scales, qzeros, g_idx):
            shifts = jnp.arange(PACK, dtype=jnp.uint32) * BITS
            qw = qweight.astype(jnp.uint32)
            w = (qw[:, None, :] >> shifts[None, :, None] & MAXQ).reshape(-1, qweight.shape[1])
            qz = qzeros.astype(jnp.uint32)
            z = ((qz[:, :, None] >> shifts[None, None, :] & MAXQ) + 1).reshape(qzeros.shape[0], -1)
            s = scales[g_idx]
            return (w.astype(scales.dtype) - z[g_idx].astype(scales.dtype)) * s
        Wg = _dequant(gate_qweight, gate_scales, gate_qzeros, gate_g_idx)
        Wu = _dequant(up_qweight, up_scales, up_qzeros, up_g_idx)
        Wd = _dequant(down_qweight, down_scales, down_qzeros, down_g_idx)
        xf = x.reshape(-1, x.shape[-1])
        h = jax.nn.silu(xf @ Wg) * (xf @ Wu)
        out = h @ Wd
        return out.reshape(x.shape[:-1] + (Wd.shape[1],))
    x = x + jnp.tanh(g_xattn[0]) * _L0_xattn_ref(_layernorm(x, axis=-1), ctx_4096, L0_xattn_Wq, L0_xattn_Wk, L0_xattn_Wv, L0_xattn_Wo)
    x = x + jnp.tanh(g_ffn[0]) * _L0_ffn_ref(_layernorm(x, axis=-1), L0_ffn_gate_qweight, L0_ffn_gate_scales, L0_ffn_gate_qzeros, L0_ffn_gate_g_idx, L0_ffn_up_qweight, L0_ffn_up_scales, L0_ffn_up_qzeros, L0_ffn_up_g_idx, L0_ffn_down_qweight, L0_ffn_down_scales, L0_ffn_down_qzeros, L0_ffn_down_g_idx)
    return x

_drawn_inputs = setup_inputs


def setup_inputs(seed=0):
    import zlib

    import numpy as np

    out = dict(_drawn_inputs(seed))
    spreads = {}
    factors = {'L0_xattn_Wq': 6.951, 'L0_xattn_Wk': 7.023}
    for name, (base, spread) in spreads.items():
        noise = np.random.default_rng([zlib.crc32(name.encode()), seed]).standard_normal(out[name].shape)
        drawn = base * np.exp(spread * noise) if base else spread * noise
        out[name] = jnp.asarray(drawn.astype(out[name].dtype))
    for name, factor in factors.items():
        out[name] = (out[name] * factor).astype(out[name].dtype)
    return out
```

```python
from contextlib import ExitStack

import concourse.bass as bass
from concourse import mybir

F32 = mybir.dt.float32
F32R = mybir.dt.float32r
I32 = mybir.dt.int32
ALU = mybir.AluOpType
ACT = mybir.ActivationFunctionType
AX = mybir.AxisListType

P = 128
BATCH, TOK, D = 8, 128, 512
HEADS, KV, HD = 16, 4, 96
GROUP = HEADS // KV
DC = D // P
PAIRS = BATCH // 2
QT = 3
TAIL = 32
INTER = 1376
NT = (INTER + P - 1) // P
LAST_N = INTER - (NT - 1) * P
SCALE = float(HD) ** -0.5
EPS = 1e-5
HIGH, LOW = 0, 1
PASSES = ((HIGH, HIGH), (HIGH, LOW), (LOW, HIGH))

PACK = 8
ZB = 2
NB = INTER // ZB
GATE_GROUPS, DOWN_GROUPS = D // P, INTER // P

SPREAD = {0: ("Q2.0", "Q2.1"), 1: ("Q2.2",), 2: ("Q3.0", "Q3.1"), 3: ("Q3.2",), 4: ("H0", "H1"), 5: ("H2", "H3")}
UNITS = 2 * KV


def ring_jobs(last):
    jobs = ["K0", "K1", "K2", "Q0.0", "Q0.1", "Q0.2", "V0", "V1", "V2", "V3", "Q1.0", "Q1.1", "Q1.2"]
    for u in range(UNITS):
        jobs += [j for j in SPREAD.get(u, ()) if not (last and j[0] == "H")] + [f"O{u}"]
    return jobs


PRO_SPLIT = 2 * QT + HEADS * HD // P + DC
PRO_JOBS = PRO_SPLIT + HEADS * HD // P
PAIR_JOBS = len(ring_jobs(False))
PAIR_SPLIT = PAIR_JOBS - UNITS


class Ring:

    def __init__(self, i, last):
        self.jobs = ring_jobs(last)
        self.split = [j for j in self.jobs if j[0] != "O"]
        self.i = i

    def bank(self, job):
        return self.jobs.index(job) % 2

    def done(self, job):
        return self.i * PAIR_JOBS + (PRO_JOBS + self.jobs.index(job) + 1)

    def slot(self, job):
        return self.i * PAIR_JOBS + (PRO_JOBS + max(self.jobs.index(job) - 1, 0))

    def high(self, job):
        return self.i * PAIR_SPLIT + (PRO_SPLIT + self.split.index(job) + 1)


def dequant_blocks(i, last):
    out = [("gate", 0, i, P), ("gate", 1, i, P), ("up", 0, i, P), ("up", 1, i, P)]
    for k in range(3):
        if last and 3 * i + k >= NT:
            continue
        rows = LAST_N if last and 3 * i + k == NT - 1 else P
        out.append(("down", 0, i * 3 + k, rows))
    return out


BLOCKS_PER_PAIR = 7


def build(nc, x, ctx, g_xattn, g_ffn, Wq, Wk, Wv, Wo, gate, up, down, out):
    quant = {"gate": gate, "up": up, "down": down}
    with ExitStack() as top:
        def sem(name):
            return top.enter_context(nc.semaphore(name))

        def sbuf(stack, name, shape, dt=F32):
            return stack.enter_context(nc.sbuf_tensor(name, shape, dt))

        x1_scratch = nc.dram_tensor("x1_scratch", (BATCH, TOK, D), F32, kind="Internal").ap()
        wgu_scratch = nc.dram_tensor("wgu_scratch", (2, DC, P, INTER), F32, kind="Internal").ap()
        wd_scratch = nc.dram_tensor("wd_scratch", (NT * P, D), F32, kind="Internal").ap()

        ps_scores = top.enter_context(nc.psum_tensor("ps_scores", [P, 2, GROUP * 256], F32))
        ps_pt = top.enter_context(nc.psum_tensor("ps_pt", [P, 2, 512], F32))
        ps_ring = top.enter_context(nc.psum_tensor("ps_ring", [P, 2, 512], F32))

        ident = sbuf(top, "ident", [P, P])
        gates = sbuf(top, "gates", [P, 2])
        tgate = sbuf(top, "tgate", [P, 2])
        neg_half = sbuf(top, "neg_half", [P, 4])
        bn = sbuf(top, "bn", [P, 4, 6])
        mv = sbuf(top, "mv", [P, 4, 2])
        veps = sbuf(top, "veps", [P, 4])
        rstd = sbuf(top, "rstd", [P, 4])


        att = ExitStack()
        wqT = sbuf(att, "wqT", [P, 2, DC, HEADS * HD], F32R)
        wkT = sbuf(att, "wkT", [P, 2, DC, KV * HD], F32R)
        wvT = sbuf(att, "wvT", [P, 2, DC, KV * HD], F32R)
        hT = sbuf(att, "hT", [P, 2, DC, 4, P], F32R)
        woT = sbuf(att, "woT", [P, KV * QT, D])
        oT = sbuf(att, "oT", [P, KV * QT, 2 * TOK])
        xin = sbuf(att, "xin", [P, 4, D])
        xres = sbuf(att, "xres", [P, 2, D])
        negmax = sbuf(att, "negmax", [P, 2, GROUP])
        sums = sbuf(att, "sums", [P, 2, GROUP])
        rsums = sbuf(att, "rsums", [P, 2, GROUP])
        gidx_i = sbuf(att, "gidx_i", [P, 2 * DC + NT], I32)
        gidx = sbuf(att, "gidx", [P, 2 * DC + NT])
        gneg = sbuf(att, "gneg", [P, 2 * DC + NT])
        idx = sbuf(att, "idx", [P, 1], I32)
        shift_row = sbuf(att, "shift_row", [P, 1], I32)
        shift_col = sbuf(att, "shift_col", [P, PACK], I32)
        rowno = sbuf(att, "rowno", [P, 1], I32)
        dq_q = sbuf(att, "dq_q", [P, NB], I32)
        dq_z = sbuf(att, "dq_z", [P, NB], I32)
        dq_zraw = sbuf(att, "dq_zraw", [P, NB // PACK], I32)
        dq_s = sbuf(att, "dq_s", [P, NB])
        with ExitStack() as raw:
            wq_raw = sbuf(raw, "wq_raw", [P, KV * QT, D])
            wk_raw = sbuf(raw, "wk_raw", [P, QT, D])
            wv_raw = sbuf(raw, "wv_raw", [P, QT, D])
            wo_raw = sbuf(raw, "wo_raw", [P, DC, KV * QT, P])
        qT = [sbuf(att, f"qT{n}", [P, 2, QT, 2 * TOK], F32R) for n in range(2)]
        q3T = [sbuf(att, f"q3T{n}", [P, 2, 2 * TOK], F32R) for n in range(2)]
        kT = sbuf(att, "kT", [P, 2, QT, 512], F32R)
        k3T = sbuf(att, "k3T", [P, 2, 512], F32R)
        v_sb = sbuf(att, "v_sb", [P, 2, 4, KV * HD], F32R)
        probs = sbuf(att, "probs", [P, 2, GROUP, 256])
        pT = sbuf(att, "pT", [P, 2, 2, 512], F32R)
        att.close()

        ffn = ExitStack()
        wgu = sbuf(ffn, "wgu", [P, 2, 2, DC, INTER], F32R)
        wd = sbuf(ffn, "wd", [P, 2, NT, D], F32R)
        x2T = sbuf(ffn, "x2T", [P, 2, DC, BATCH * TOK], F32R)
        hidden = sbuf(ffn, "hidden", [P, 2, 2, 512], F32R)
        silu = sbuf(ffn, "silu", [P, 2, 512])
        x1t = sbuf(ffn, "x1t", [P, 2, D])
        yt = sbuf(ffn, "yt", [P, 2, D])
        st_gu = sbuf(ffn, "st_gu", [P, 2, 2, DC, P])
        st_d = sbuf(ffn, "st_d", [P, 2, D])
        ffn.close()

        const_ready = sem("const_ready")
        shifts_ready = sem("shifts_ready")
        wk_in, wv_in, wo_in = sem("wk_in"), sem("wv_in"), sem("wo_in")
        wq_in = sem("wq_in")
        small_in = sem("small_in")
        x_in = sem("x_in")
        ln_stat = sem("ln_stat")
        ln_var = sem("ln_var")
        ln_rstd = sem("ln_rstd")
        ln_done = sem("ln_done")
        tanh_done = sem("tanh_done")
        ring_full, ring_high, ring_free = sem("ring_full"), sem("ring_high"), sem("ring_free")
        k3_in = sem("k3_in")
        q3_in = [sem("q3_in0"), sem("q3_in1")]
        s_full, maxed, expd, recip, normed = (sem(n) for n in ("s_full", "maxed", "expd", "recip", "normed"))
        pt_full, pt_high, pt_low = sem("pt_full"), sem("pt_high"), sem("pt_low")
        y_full, y_free = sem("y_full"), sem("y_free")
        xres_in, x1_out = sem("xres_in"), sem("x1_out")
        gi_chain = sem("gi_chain")
        idx_ready, gathered, q_in, unpacked, w_ready, w_out, dq_chain = (
            sem(n) for n in ("idx_ready", "gathered", "q_in", "unpacked", "w_ready", "w_out", "dq_chain"))
        stage_in = [sem("stage_in0"), sem("stage_in1")]
        w_high, w_low = sem("w_high"), sem("w_low")
        passed_v, passed_p = sem("passed_v"), sem("passed_p")
        x1_in = [sem("x1_in0"), sem("x1_in1")]
        f_stat, f_mv, f_var, f_rstd, f_ln = (sem(n) for n in ("f_stat", "f_mv", "f_var", "f_rstd", "f_ln"))
        xt_full, xt_high, xt_low = sem("xt_full"), sem("xt_high"), sem("xt_low")
        g_full, u_full, silu_done, h_done, h_high, h_low, down_done = (
            sem(n) for n in ("g_full", "u_full", "silu_done", "h_done", "h_high", "h_low", "down_done"))
        f_y_full, f_y_free = sem("f_y_full"), sem("f_y_free")
        res_in = [sem("res_in0"), sem("res_in1")]
        o_out = [sem("o_out0"), sem("o_out1")]

        block = top.enter_context(nc.Block())

        def in_rows(src, i):
            return src[bass.ds(i * 2, 2)].rearrange("b p d -> p b d")

        @block.sync
        def _(sp):
            sp.dma_start(xin[:, 0:2, :], in_rows(x, 0)).then_inc(x_in, 16)
            sp.dma_start(xin[:, 2:4, :], in_rows(ctx, 0)).then_inc(x_in, 16)
            sp.dma_start(wk_raw[0:HD], Wk[0:QT * HD].rearrange("(j p) d -> p j d", p=HD)).then_inc(wk_in, 16)
            sp.dma_start(wk_raw[HD:P], Wk[QT * HD:].rearrange("(j p) d -> p j d", p=TAIL)).then_inc(wk_in, 16)
            sp.dma_start(wv_raw[:], Wv.rearrange("(j p) d -> p j d", p=P)).then_inc(wv_in, 16)
            for kv in range(KV):
                rows, dst = Wq[kv * GROUP * HD:(kv + 1) * GROUP * HD], wq_raw[:, kv * QT:(kv + 1) * QT]
                sp.dma_start(dst[0:HD], rows[0:QT * HD].rearrange("(j p) d -> p j d", p=HD)).then_inc(wq_in, 16)
                sp.dma_start(dst[HD:P], rows[QT * HD:].rearrange("(j p) d -> p j d", p=TAIL)).then_inc(wq_in, 16)
            for b in range(DC):
                cols = Wo[b * P:(b + 1) * P].rearrange("p (k c) -> p k c", k=KV)
                dst = wo_raw[:, b].rearrange("p (k j) e -> p k j e", k=KV)
                for kv in range(KV):
                    sp.dma_start(dst[:, kv, :, 0:HD], cols[:, kv, 0:QT * HD].rearrange("p (j e) -> p j e", j=QT)).then_inc(wo_in, 16)
                    sp.dma_start(dst[:, kv, :, HD:P], cols[:, kv, QT * HD:].rearrange("p (j e) -> p j e", j=QT)).then_inc(wo_in, 16)

            sp.dma_start(xres[:], in_rows(x, 0)).then_inc(xres_in, 16)

            def raw_block(i, last, k):
                name, cb, t, rows = dequant_blocks(i, last)[k]
                qw = quant[name][0]
                width, cols = (NB, INTER) if name != "down" else (D, D)
                first = i * BLOCKS_PER_PAIR + k
                if k > 0 or last:
                    sp.wait_ge(w_out, first * 16)
                src = bass.AP(qw.tensor, t * (P // PACK * cols) + cb * NB, [[cols, rows // PACK], [0, PACK], [1, width]])
                sp.dma_start(dq_q[0:rows, 0:width], src).then_inc(q_in, 16)

            def store_block(i, last, k):
                name, cb, t, rows = dequant_blocks(i, last)[k]
                sp.wait_ge(w_ready, i * BLOCKS_PER_PAIR + (k + 1))
                if name == "down":
                    dst = wd_scratch[bass.ds(t * P, rows)]
                    sp.dma_start(dst, dq_q[0:rows, 0:D].bitcast(F32)).then_inc(w_out, 16)
                else:
                    dst = wgu_scratch[("gate", "up").index(name)].rearrange("c p n -> (c p) n")
                    sp.dma_start(dst[bass.ds(t * P, P), cb * NB:(cb + 1) * NB], dq_q[:].bitcast(F32)).then_inc(w_out, 16)

            def body(i, last):
                ring = Ring(i, last)
                blocks = len(dequant_blocks(i, last))
                if not last:
                    sp.wait_ge(ring_full, i * PAIR_JOBS + PRO_JOBS)
                    sp.dma_start(xin[:, 0:2, :], in_rows(x, i + 1)).then_inc(x_in, 16)
                    sp.dma_start(xin[:, 2:4, :], in_rows(ctx, i + 1)).then_inc(x_in, 16)

                def tails(dst, src, done, width):
                    for j in range(QT):
                        sp.dma_start(dst[TAIL * j:TAIL * (j + 1), :, 0:width].bitcast(F32), src[HD:P, :, j, 0:width].bitcast(F32)).then_inc(done, 16)

                sp.wait_ge(ring_free, ring.done("K2"))
                tails(k3T, kT, k3_in, 512)
                sp.wait_ge(ring_free, ring.done("Q0.2"))
                tails(q3T[0], qT[0], q3_in[0], 2 * TOK)
                sp.wait_ge(ring_free, ring.done("Q1.2"))
                tails(q3T[1], qT[1], q3_in[1], 2 * TOK)
                raw_block(i, last, 0)
                for u in range(UNITS):
                    if u in (1, 3):
                        kv = (u + 3) // 2
                        sp.wait_ge(ring_free, ring.done(f"Q{kv}.2"))
                        tails(q3T[kv % 2], qT[kv % 2], q3_in[kv % 2], 2 * TOK)
                    if 1 <= u <= blocks:
                        store_block(i, last, u - 1)
                        if u < blocks:
                            raw_block(i, last, u)
                for b in range(2):
                    sp.wait_ge(y_free, i * 2 + (b + 1))
                    sp.dma_start(x1_scratch[bass.ds(i * 2 + b, 1)].rearrange("b p d -> (b p) d"), xres[:, b]).then_inc(x1_out, 16)
                if not last:
                    sp.wait_ge(x1_out, i * 32 + 32)
                    sp.dma_start(xres[:], in_rows(x, i + 1)).then_inc(xres_in, 16)

            with sp.Fori(0, PAIRS - 1, 1) as i:
                body(i, False)
            body(PAIRS - 1, True)

            sp.wait_ge(x1_out, PAIRS * 32)
            sp.wait_ge(w_out, 16 * (BLOCKS_PER_PAIR * PAIRS - 1))

            def load_x1(m):
                if m >= 2:
                    sp.wait_ge(xt_full, m - 1)
                sp.dma_start(x1t[:, m % 2], x1_scratch[m]).then_inc(x1_in[m % 2], 16)

            def load_w(n):
                w = P if n < NT - 1 else LAST_N
                if n >= 2:
                    sp.wait_ge(w_low, n - 1)
                for m in range(2):
                    src = wgu_scratch[m, :, :, n * P:n * P + w].rearrange("c p n -> p c n")
                    sp.dma_start(st_gu[:, n % 2, m, :, 0:w], src).then_inc(stage_in[n % 2], 16)
                sp.dma_start(st_d[0:w, n % 2], wd_scratch[n * P:n * P + w]).then_inc(stage_in[n % 2], 16)

            load_x1(0)
            load_x1(1)
            load_w(0)
            load_w(1)
            for m in range(2, BATCH):
                load_x1(m)
            for n in range(2, NT):
                load_w(n)
            for m in range(BATCH):
                if m < 2:
                    sp.wait_ge(f_ln, BATCH)
                    sp.wait_ge(xt_full, BATCH)
                else:
                    sp.wait_ge(f_y_free, m - 1)
                    sp.wait_ge(o_out[m % 2], 16 * (m // 2))
                sp.dma_start(x1t[:, m % 2], x1_scratch[m]).then_inc(res_in[m % 2], 16)
                sp.wait_ge(f_y_free, m + 1)
                sp.dma_start(out[m], yt[:, m % 2]).then_inc(o_out[m % 2], 16)
            for n in range(2):
                sp.wait_ge(o_out[n], 16 * (BATCH // 2))

        @block.gpsimd
        def _(pool):
            nc.gpsimd.memset(ident[:], 0.0).then_inc(const_ready, 1)
            pool.wait_ge(const_ready, 1)
            nc.gpsimd.affine_select(out=ident[:], in_=ident[:], compare_op=ALU.not_equal, fill=1.0, base=0,
                                    pattern=[[-1, P]], channel_multiplier=1).then_inc(const_ready, 1)
            nc.gpsimd.memset(neg_half[:], -0.5).then_inc(const_ready, 1)
            nc.gpsimd.iota(rowno[:], pattern=[[0, 1]], base=0, channel_multiplier=1).then_inc(const_ready, 1)
            nc.gpsimd.iota(shift_col[:], pattern=[[4, PACK]], base=0, channel_multiplier=0).then_inc(const_ready, 1)

            def ln_power(n):
                pool.wait_ge(ln_var, n)
                nc.gpsimd.tensor_tensor(out=rstd[:, 0:2], in0=veps[:, 0:2], in1=neg_half[:, 0:2], op=ALU.pow).then_inc(ln_rstd, 1)

            def carry():
                pool.sem_inc(passed_p, 1)

            def normalise(i, u):
                pool.wait_ge(recip, i * UNITS + (u + 1))
                carry()
                for h in range(GROUP):
                    op = nc.gpsimd.tensor_scalar(probs[:, u % 2, h], probs[:, u % 2, h], rsums[:, u % 2, h:h + 1], 1.0,
                                                 ALU.mult, ALU.mult)
                op.then_inc(normed, 1)

            def gather(i, last, k):
                name, cb, t, rows = dequant_blocks(i, last)[k]
                _, scales, zeros, _ = quant[name]
                width, split = (NB, ZB) if name != "down" else (D, 1)
                pool.wait_ge(idx_ready, i * BLOCKS_PER_PAIR + (k + 1))
                if k > 0 or last:
                    pool.wait_ge(w_ready, i * BLOCKS_PER_PAIR + k)
                carry()
                at = bass.IndirectOffsetOnAxis(ap=idx[0:rows, 0:1], axis=0)
                nc.gpsimd.indirect_dma_start(dq_s[0:rows, 0:width], None, scales.rearrange("g (b n) -> (g b) n", b=split), at).then_inc(gathered, 16)
                nc.gpsimd.indirect_dma_start(dq_zraw[0:rows, 0:width // PACK], None, zeros.rearrange("g (b n) -> (g b) n", b=split), at).then_inc(gathered, 16)

            def rescale(i, last, k):
                name, cb, t, rows = dequant_blocks(i, last)[k]
                width = NB if name != "down" else D
                pool.wait_ge(unpacked, i * BLOCKS_PER_PAIR + (k + 1))
                w = dq_q[0:rows, 0:width].bitcast(F32)
                nc.gpsimd.tensor_tensor(out=w, in0=w, in1=dq_s[0:rows, 0:width], op=ALU.mult).then_inc(w_ready, 1)

            pool.wait_ge(const_ready, 3)
            ln_power(1)

            def body(i, last):
                blocks = len(dequant_blocks(i, last))
                normalise(i, 0)
                normalise(i, 1)
                for u in range(UNITS):
                    if u < blocks:
                        gather(i, last, u)
                    if u == 1 and not last:
                        ln_power(i + 2)
                    if u + 2 < UNITS:
                        normalise(i, u + 2)
                    if u < blocks:
                        rescale(i, last, u)

            with pool.Fori(0, PAIRS - 1, 1) as i:
                body(i, False)
            body(PAIRS - 1, True)
            for m in range(BATCH):
                pool.wait_ge(f_var, m + 1)
                nc.gpsimd.tensor_tensor(out=rstd[:, m % 2:m % 2 + 1], in0=veps[:, m % 2:m % 2 + 1],
                                        in1=neg_half[:, 0:1], op=ALU.pow).then_inc(f_rstd, 1)

        @block.scalar
        def _(act):
            act.dma_start(gates[:, 0:1], bass.AP(g_xattn.tensor, 0, [[0, P], [1, 1]])).then_inc(small_in, 16)
            act.dma_start(gates[:, 1:2], bass.AP(g_ffn.tensor, 0, [[0, P], [1, 1]])).then_inc(small_in, 16)
            act.wait_ge(gi_chain, 1)
            act.dma_start(gidx_i[:, 0:DC], gate[3].rearrange("(c p) -> p c", p=P), allow_slow_non_contiguous=True).then_inc(small_in, 16)
            act.dma_start(gidx_i[:, DC:2 * DC], up[3].rearrange("(c p) -> p c", p=P), allow_slow_non_contiguous=True).then_inc(small_in, 16)
            act.dma_start(gidx_i[:, 2 * DC:2 * DC + NT - 1],
                           down[3][0:(NT - 1) * P].rearrange("(c p) -> p c", p=P), allow_slow_non_contiguous=True).then_inc(small_in, 16)
            act.dma_start(gidx_i[0:LAST_N, 2 * DC + NT - 1:], down[3][(NT - 1) * P:].rearrange("(c p) -> p c", c=1), allow_slow_non_contiguous=True).then_inc(small_in, 16)
            act.wait_ge(small_in, 96)
            nc.scalar.activation(tgate[:], gates[:], ACT.Tanh).then_inc(tanh_done, 1)

            def high(job_done, bank, dst, cols=512, rows=P, shape=None, scale=1.0):
                act.wait_ge(ring_full, job_done)
                src = ps_ring[0:rows, bank, 0:cols]
                if shape:
                    src = src.rearrange(*shape[0], **shape[1])
                nc.scalar.activation(dst, src, ACT.Copy, scale=scale).then_inc(ring_high, 1)

            by_chunk = (("p (c n) -> p c n",), {"c": DC})
            for job in range(2 * QT + HEADS * HD // P):
                dst, t = (wkT, job) if job < QT else (wvT, job - QT) if job < 2 * QT else (wqT, job - 2 * QT)
                high(job + 1, job % 2, dst[:, HIGH, :, t * P:(t + 1) * P], shape=by_chunk)
            for m in range(DC):
                job = PRO_JOBS - DC + m
                high(job + 1, job % 2, hT[:, HIGH, :, m, :], shape=by_chunk)

            def body(i, last):
                ring = Ring(i, last)

                def evacuate(job):
                    done, bank = ring.done(job), ring.bank(job)
                    if job[0] == "K":
                        dst = kT[:, HIGH, int(job[1])].rearrange("p (b t s) -> p t b s", b=2, t=2)
                        high(done, bank, dst, shape=(("p (t b s) -> p t b s",), {"b": 2, "t": 2}))
                    elif job[0] == "V":
                        high(done, bank, v_sb[:, HIGH, int(job[1])], KV * HD)
                    elif job[0] == "Q":
                        high(done, bank, qT[int(job[1]) % 2][:, HIGH, int(job[3])], 2 * TOK, scale=SCALE)
                    else:
                        high(done, bank, hT[:, HIGH, :, int(job[1]), :], shape=by_chunk)

                def exponentials(u):
                    act.wait_ge(maxed, i * UNITS + (u + 1))
                    for h in range(GROUP):
                        op = nc.scalar.activation(probs[:, u % 2, h], ps_scores[:, u % 2, h * 256:(h + 1) * 256], ACT.Exp,
                                                  bias=negmax[:, u % 2, h:h + 1], accum_out=sums[:, u % 2, h:h + 1])
                    op.then_inc(expd, 1)

                for job in ("K0", "K1", "K2", "Q0.0", "Q0.1", "Q0.2"):
                    evacuate(job)
                exponentials(0)
                evacuate("V0")
                evacuate("V1")
                exponentials(1)
                for job in ("V2", "V3", "Q1.0", "Q1.1", "Q1.2"):
                    evacuate(job)
                for u in range(UNITS):
                    for t in range(2):
                        act.wait_ge(pt_full, i * (2 * UNITS) + (2 * u + t + 1))
                        nc.scalar.activation(pT[:, HIGH, t], ps_pt[:, t], ACT.Copy).then_inc(pt_high, 1)
                    if u + 2 < UNITS:
                        exponentials(u + 2)
                    for job in SPREAD.get(u, ()):
                        if not (last and job[0] == "H"):
                            evacuate(job)

            with act.Fori(0, PAIRS - 1, 1) as i:
                body(i, False)
            body(PAIRS - 1, True)

            act.wait_ge(y_full, 2 * PAIRS)
            act.wait_ge(y_free, 2 * PAIRS)

            def split_w(n):
                w = P if n < NT - 1 else LAST_N
                act.wait_ge(stage_in[n % 2], 48 * (n // 2 + 1))
                for m in range(2):
                    nc.scalar.activation(wgu[:, HIGH, m, :, n * P:n * P + w], st_gu[:, n % 2, m, :, 0:w], ACT.Copy)
                nc.scalar.activation(wd[0:w, HIGH, n], st_d[0:w, n % 2], ACT.Copy).then_inc(w_high, 1)

            split_w(0)
            for m in range(BATCH):
                act.wait_ge(xt_full, m + 1)
                bank = ps_pt[:, m % 4] if m % 4 < 2 else ps_ring[:, m % 4 - 2]
                nc.scalar.activation(x2T[:, HIGH, :, m * P:(m + 1) * P], bank.rearrange("p (c n) -> p c n", c=DC),
                                     ACT.Copy).then_inc(xt_high, 1)
            split_w(1)
            for hf in range(2):
                for n in range(NT):
                    w, at = (P if n < NT - 1 else LAST_N), hf * NT + n
                    act.wait_ge(g_full, at + 1)
                    if at >= 2:
                        act.wait_ge(h_low, at - 1)
                    nc.scalar.activation(silu[0:w, at % 2], ps_scores[0:w, at % 2, 0:512], ACT.Silu).then_inc(silu_done, 1)
                    if hf == 0 and n + 2 < NT:
                        split_w(n + 2)
                    act.wait_ge(h_done, at + 1)
                    if at >= 2:
                        act.wait_ge(down_done, at - 1)
                    nc.scalar.activation(hidden[0:w, at % 2, HIGH], silu[0:w, at % 2], ACT.Copy).then_inc(h_high, 1)

        @block.vector
        def _(dve):
            nc.vector.memset(gidx_i[:], 0).then_inc(gi_chain, 1)

            def layer_norm(i_next, wait_in):
                dve.wait_ge(x_in, wait_in)
                for m in range(2):
                    nc.vector.bn_stats(bn[:, m], xin[:, m]).then_inc(ln_stat, 1)
                base = i_next * 5
                dve.wait_ge(ln_stat, base + 2)
                dve.sem_inc(passed_v, 1)
                for m in range(2):
                    nc.vector.bn_aggr(mv[:, m], bn[:, m]).then_inc(ln_stat, 1)
                dve.wait_ge(ln_stat, base + 4)
                nc.vector.tensor_scalar(veps[:, 0:2], mv[:, 0:2, 1], EPS, None, ALU.add).then_inc(ln_var, 1)

            def layer_norm_apply(i_next):
                dve.wait_ge(ln_rstd, i_next + 1)
                for m in range(2):
                    op = nc.vector.tensor_scalar(xin[:, m], xin[:, m], mv[:, m, 0:1], rstd[:, m:m + 1], ALU.subtract, ALU.mult)
                op.then_inc(ln_done, 1)
                nc.vector.memset(bn[:, 3], 0.0).then_inc(ln_stat, 1)

            def low(high_done, bank, dst, hi, cols=512, shape=None, scale=None):
                dve.wait_ge(ring_high, high_done)
                src = ps_ring[:, bank, 0:cols]
                if shape:
                    src = src.rearrange(*shape[0], **shape[1])
                if scale is None:
                    nc.vector.tensor_tensor(dst, src, hi.bitcast(F32), ALU.subtract).then_inc(ring_free, 1)
                else:
                    nc.vector.scalar_tensor_tensor(out=dst, in0=src, scalar=scale, in1=hi.bitcast(F32), op0=ALU.mult,
                                                   op1=ALU.subtract).then_inc(ring_free, 1)

            dve.wait_ge(const_ready, 5)
            nc.vector.tensor_scalar(shift_row[:], rowno[:], PACK - 1, 2, ALU.bitwise_and, ALU.logical_shift_left).then_inc(shifts_ready, 1)
            by_chunk = (("p (c n) -> p c n",), {"c": DC})
            layer_norm(0, 32)
            for job in range(2 * QT + HEADS * HD // P):
                dst, t = (wkT, job) if job < QT else (wvT, job - QT) if job < 2 * QT else (wqT, job - 2 * QT)
                low(job + 1, job % 2, dst[:, LOW, :, t * P:(t + 1) * P], dst[:, HIGH, :, t * P:(t + 1) * P], shape=by_chunk)
                if job == 2:
                    layer_norm_apply(0)
            first = 2 * QT + HEADS * HD // P
            for t in range(KV * QT):
                job = first + t
                dve.wait_ge(ring_full, job + 1)
                nc.vector.tensor_copy(woT[:, t], ps_ring[:, job % 2]).then_inc(ring_free, 1)
            for m in range(DC):
                job = PRO_JOBS - DC + m
                low(first + m + 1, job % 2, hT[:, LOW, :, m, :], hT[:, HIGH, :, m, :], shape=by_chunk)

            dve.wait_ge(small_in, 96)
            nc.vector.tensor_copy(gidx[:], gidx_i[:]).then_inc(gi_chain, 1)
            dve.wait_ge(gi_chain, 2)
            for cols, groups in ((slice(0, 2 * DC), GATE_GROUPS), (slice(2 * DC, 2 * DC + NT), DOWN_GROUPS)):
                nc.vector.tensor_scalar(gneg[:, cols], gidx[:, cols], 0.0, float(groups), ALU.is_lt, ALU.mult).then_inc(gi_chain, 1)
            dve.wait_ge(gi_chain, 4)
            nc.vector.tensor_tensor(gidx[:], gidx[:], gneg[:], ALU.add).then_inc(gi_chain, 1)
            dve.wait_ge(gi_chain, 5)
            for cols, groups in ((slice(0, 2 * DC), GATE_GROUPS), (slice(2 * DC, 2 * DC + NT), DOWN_GROUPS)):
                nc.vector.tensor_scalar(gidx[:, cols], gidx[:, cols], 0.0, float(groups - 1), ALU.max, ALU.min).then_inc(gi_chain, 1)
            dve.wait_ge(gi_chain, 7)
            dve.wait_ge(shifts_ready, 1)
            dve.wait_ge(tanh_done, 1)

            def indices(i, last, k):
                name, cb, t, rows = dequant_blocks(i, last)[k]
                col = {"gate": 0, "up": DC, "down": 2 * DC}[name] + t
                split = ZB if name != "down" else 1
                nc.vector.tensor_scalar(idx[:], gidx[:, bass.ds(col, 1)], float(split), float(cb), ALU.mult, ALU.add).then_inc(idx_ready, 1)

            def unpack(i, last, k):
                name, cb, t, rows = dequant_blocks(i, last)[k]
                width = NB if name != "down" else D
                n = i * BLOCKS_PER_PAIR + (k + 1)
                dve.wait_ge(gathered, n * 32)
                z = dq_z[0:rows, 0:width]
                nc.vector.tensor_tensor(z.rearrange("p (c j) -> p c j", j=PACK),
                                        dq_zraw[0:rows, 0:width // PACK].unsqueeze(2).to_broadcast([rows, width // PACK, PACK]),
                                        shift_col[0:rows].unsqueeze(1).to_broadcast([rows, width // PACK, PACK]),
                                        ALU.logical_shift_right).then_inc(dq_chain, 1)
                dve.wait_ge(q_in, n * 16)
                q = dq_q[0:rows, 0:width]
                nc.vector.tensor_scalar(q, q, shift_row[0:rows, 0:1], PACK * 2 - 1, ALU.logical_shift_right,
                                        ALU.bitwise_and).then_inc(dq_chain, 1)
                dve.wait_ge(dq_chain, i * (3 * BLOCKS_PER_PAIR) + (3 * k + 1))
                nc.vector.tensor_scalar(z, z, PACK * 2 - 1, None, ALU.bitwise_and).then_inc(dq_chain, 1)
                dve.wait_ge(dq_chain, i * (3 * BLOCKS_PER_PAIR) + (3 * k + 3))
                nc.vector.scalar_tensor_tensor(out=q.bitcast(F32), in0=q, scalar=1.0, in1=z, op0=ALU.subtract,
                                               op1=ALU.subtract).then_inc(unpacked, 1)

            def body(i, last):
                ring = Ring(i, last)
                blocks = len(dequant_blocks(i, last))

                def evacuate(job):
                    done, bank = ring.high(job), ring.bank(job)
                    if job[0] == "K":
                        def dst(part):
                            return kT[:, part, int(job[1])].rearrange("p (b t s) -> p t b s", b=2, t=2)
                        low(done, bank, dst(LOW), dst(HIGH), shape=(("p (t b s) -> p t b s",), {"b": 2, "t": 2}))
                    elif job[0] == "V":
                        low(done, bank, v_sb[:, LOW, int(job[1])], v_sb[:, HIGH, int(job[1])], KV * HD)
                    elif job[0] == "Q":
                        q = qT[int(job[1]) % 2]
                        low(done, bank, q[:, LOW, int(job[3])], q[:, HIGH, int(job[3])], 2 * TOK, scale=SCALE)
                    else:
                        low(done, bank, hT[:, LOW, :, int(job[1]), :], hT[:, HIGH, :, int(job[1]), :], shape=by_chunk)

                def maxima(u):
                    dve.wait_ge(s_full, i * UNITS + (u + 1))
                    nc.vector.tensor_reduce(negmax[:, u % 2], ps_scores[:, u % 2].rearrange("p (h s) -> p h s", h=GROUP),
                                            AX.X, ALU.max, negate=True).then_inc(maxed, 1)

                def reciprocals(u):
                    dve.wait_ge(expd, i * UNITS + (u + 1))
                    nc.vector.reciprocal(rsums[:, u % 2], sums[:, u % 2]).then_inc(recip, 1)

                def attention_out(u):
                    kv, b = u // 2, u % 2
                    dve.wait_ge(ring_full, ring.done(f"O{u}"))
                    o = ps_ring[0:HD, ring.bank(f"O{u}")].rearrange("p (h q) -> p h q", h=GROUP)
                    tiles = oT[:, kv * QT:(kv + 1) * QT, b * TOK:(b + 1) * TOK]
                    for j in range(QT):
                        nc.vector.tensor_copy(tiles[HD:P, j], o[TAIL * j:TAIL * (j + 1), GROUP - 1])
                    nc.vector.tensor_copy(tiles[0:HD], o[:, 0:QT]).then_inc(ring_free, 1)

                for job in ("K0", "K1", "K2", "Q0.0", "Q0.1", "Q0.2"):
                    evacuate(job)
                maxima(0)
                maxima(1)
                evacuate("V0")
                reciprocals(0)
                evacuate("V1")
                reciprocals(1)
                for job in ("V2", "V3", "Q1.0", "Q1.1", "Q1.2"):
                    evacuate(job)
                for u in range(UNITS):
                    for t in range(2):
                        dve.wait_ge(pt_high, i * (2 * UNITS) + (2 * u + t + 1))
                        nc.vector.tensor_tensor(pT[:, LOW, t], ps_pt[:, t], pT[:, HIGH, t].bitcast(F32), ALU.subtract).then_inc(pt_low, 1)
                    if u + 2 < UNITS:
                        maxima(u + 2)
                    if u < blocks:
                        indices(i, last, u)
                    for job in SPREAD.get(u, ()):
                        if not (last and job[0] == "H"):
                            evacuate(job)
                    if u == 1 and not last:
                        layer_norm(i + 1, i * 32 + 64)
                    if u + 2 < UNITS:
                        reciprocals(u + 2)
                    if u == 2 and not last:
                        layer_norm_apply(i + 1)
                    if u < blocks:
                        unpack(i, last, u)
                    attention_out(u)
                dve.wait_ge(xres_in, i * 16 + 16)
                for b in range(2):
                    dve.wait_ge(y_full, i * 2 + (b + 1))
                    nc.vector.scalar_tensor_tensor(out=xres[:, b], in0=ps_scores[:, b, 0:D], scalar=tgate[:, 0:1],
                                                   in1=xres[:, b], op0=ALU.mult, op1=ALU.add).then_inc(y_free, 1)

            with dve.Fori(0, PAIRS - 1, 1) as i:
                body(i, False)
            body(PAIRS - 1, True)

            dve.wait_ge(y_full, 2 * PAIRS)
            dve.wait_ge(y_free, 2 * PAIRS)

            def split_w(n):
                w = P if n < NT - 1 else LAST_N
                dve.wait_ge(w_high, n + 1)
                for m in range(2):
                    nc.vector.tensor_tensor(wgu[:, LOW, m, :, n * P:n * P + w], st_gu[:, n % 2, m, :, 0:w],
                                            wgu[:, HIGH, m, :, n * P:n * P + w].bitcast(F32), ALU.subtract)
                nc.vector.tensor_tensor(wd[0:w, LOW, n], st_d[0:w, n % 2], wd[0:w, HIGH, n].bitcast(F32),
                                        ALU.subtract).then_inc(w_low, 1)

            def x2_low(m):
                dve.wait_ge(xt_high, m + 1)
                bank = ps_pt[:, m % 4] if m % 4 < 2 else ps_ring[:, m % 4 - 2]
                cols = slice(m * P, (m + 1) * P)
                nc.vector.tensor_tensor(x2T[:, LOW, :, cols], bank.rearrange("p (c n) -> p c n", c=DC),
                                        x2T[:, HIGH, :, cols].bitcast(F32), ALU.subtract).then_inc(xt_low, 1)

            for m in range(BATCH):
                s = m % 2
                dve.wait_ge(x1_in[s], 16 * (m // 2 + 1))
                nc.vector.bn_stats(bn[:, s], x1t[:, s]).then_inc(f_stat, 1)
                dve.wait_ge(f_stat, m + 1)
                nc.vector.bn_aggr(mv[:, s], bn[:, s]).then_inc(f_mv, 1)
                dve.wait_ge(f_mv, m + 1)
                nc.vector.tensor_scalar(veps[:, s:s + 1], mv[:, s, 1:2], EPS, None, ALU.add).then_inc(f_var, 1)
                if m == 0:
                    split_w(0)
                else:
                    x2_low(m - 1)
                dve.wait_ge(f_rstd, m + 1)
                nc.vector.tensor_scalar(x1t[:, s], x1t[:, s], mv[:, s, 0:1], rstd[:, s:s + 1], ALU.subtract,
                                        ALU.mult).then_inc(f_ln, 1)
            x2_low(BATCH - 1)
            split_w(1)
            for hf in range(2):
                for n in range(NT):
                    w, at = (P if n < NT - 1 else LAST_N), hf * NT + n
                    dve.wait_ge(silu_done, at + 1)
                    dve.wait_ge(u_full, at + 1)
                    nc.vector.tensor_tensor(silu[0:w, at % 2], ps_scores[0:w, at % 2, 512:1024], silu[0:w, at % 2], ALU.mult).then_inc(h_done, 1)
                    if hf == 0 and n + 2 < NT:
                        split_w(n + 2)
                    dve.wait_ge(h_high, at + 1)
                    nc.vector.tensor_tensor(hidden[0:w, at % 2, LOW], silu[0:w, at % 2],
                                            hidden[0:w, at % 2, HIGH].bitcast(F32), ALU.subtract).then_inc(h_low, 1)
                for m in range(4):
                    at = hf * 4 + m
                    dve.wait_ge(f_y_full, at + 1)
                    dve.wait_ge(res_in[at % 2], 16 * (at // 2 + 1))
                    bank = ps_pt[:, m] if m < 2 else ps_ring[:, m - 2]
                    nc.vector.scalar_tensor_tensor(out=yt[:, at % 2], in0=bank, scalar=tgate[:, 1:2], in1=x1t[:, at % 2],
                                                   op0=ALU.mult, op1=ALU.add).then_inc(f_y_free, 1)

        @block.tensor
        def _(pe):
            pe.wait_ge(const_ready, 2)

            def transpose_job(job, tiles):
                if job >= 2:
                    pe.wait_ge(ring_free, job - 1)
                for c, t in enumerate(tiles):
                    op = nc.tensor.transpose(ps_ring[:, job % 2, c * P:(c + 1) * P], t, ident[:])
                op.then_inc(ring_full, 1)

            pe.wait_ge(wk_in, 32)
            for t in range(QT):
                transpose_job(t, [wk_raw[:, t, c * P:(c + 1) * P] for c in range(DC)])
            pe.wait_ge(wv_in, 16)
            for t in range(QT):
                transpose_job(QT + t, [wv_raw[:, t, c * P:(c + 1) * P] for c in range(DC)])
            pe.wait_ge(wq_in, 32 * KV)
            for t in range(KV * QT):
                transpose_job(2 * QT + t, [wq_raw[:, t, c * P:(c + 1) * P] for c in range(DC)])
            pe.wait_ge(wo_in, 32 * KV * DC)
            for t in range(KV * QT):
                transpose_job(2 * QT + KV * QT + t, [wo_raw[:, b, t] for b in range(DC)])
            pe.wait_ge(ln_done, 1)
            pe.wait_ge(x_in, 32)
            for m in range(DC):
                transpose_job(PRO_JOBS - DC + m, [xin[:, m, c * P:(c + 1) * P] for c in range(DC)])

            def body(i, last):
                ring = Ring(i, last)

                def open_slot(job):
                    pe.wait_ge(ring_free, ring.slot(job))
                    return ps_ring[:, ring.bank(job)]

                def product(dst, stationary, moving):
                    for c in range(DC):
                        for n, (a, b) in enumerate(PASSES):
                            op = nc.tensor.matmul(dst, stationary(a, c), moving(b, c), start=(c == 0 and n == 0),
                                                  stop=(c == DC - 1 and n == len(PASSES) - 1))
                    return op

                def project(job):
                    bank = open_slot(job)
                    if job[0] == "K":
                        cols = slice(int(job[1]) * P, (int(job[1]) + 1) * P)
                        op = product(bank, lambda a, c: wkT[:, a, c, cols], lambda b, c: hT[:, b, c])
                    elif job[0] == "V":
                        m = int(job[1])
                        op = product(bank[:, 0:KV * HD], lambda a, c: hT[:, a, c, m], lambda b, c: wvT[:, b, c])
                    elif job[0] == "Q":
                        t = int(job[1]) * QT + int(job[3])
                        op = product(bank[:, 0:2 * TOK], lambda a, c: wqT[:, a, c, t * P:(t + 1) * P],
                                     lambda b, c: hT[:, b, c, 0:2])
                    else:
                        m = int(job[1])
                        if m == 0:
                            pe.wait_ge(ln_done, i + 2)
                            pe.wait_ge(x_in, i * 32 + 64)
                        for c in range(DC):
                            op = nc.tensor.transpose(bank[:, c * P:(c + 1) * P], xin[:, m, c * P:(c + 1) * P], ident[:])
                    op.then_inc(ring_full, 1)

                def scores(u):
                    kv, b = u // 2, u % 2
                    if u == 0:
                        pe.wait_ge(ring_free, ring.done("Q0.2"))
                    if b == 0:
                        pe.wait_ge(ring_free, ring.done(f"Q{kv}.2"))
                    if u >= 2:
                        pe.wait_ge(expd, i * UNITS + (u - 1))
                    if kv == KV - 1 and b == 0:
                        pe.wait_ge(k3_in, i * 48 + 48)
                    q = slice(b * TOK, (b + 1) * TOK)
                    s = slice(b * 256, (b + 1) * 256)
                    for h in range(GROUP):
                        if h == GROUP - 1 and b == 0:
                            pe.wait_ge(q3_in[kv % 2], i * 96 + (kv // 2 + 1) * 48)
                        for n, (pa, pb) in enumerate(PASSES):
                            stat = qT[kv % 2][0:HD, pa, h, q] if h < QT else q3T[kv % 2][0:HD, pa, q]
                            mov = kT[0:HD, pb, kv, s] if kv < QT else k3T[0:HD, pb, s]
                            op = nc.tensor.matmul(ps_scores[:, b, h * 256:(h + 1) * 256], stat, mov, start=(n == 0),
                                                  stop=(n == len(PASSES) - 1), skip_group_check=True)
                    op.then_inc(s_full, 1)

                def transpose_probs(u):
                    pe.wait_ge(normed, i * UNITS + (u + 1))
                    for t in range(2):
                        for h in range(GROUP):
                            op = nc.tensor.transpose(ps_pt[:, t, h * P:(h + 1) * P], probs[:, u % 2, h, t * P:(t + 1) * P], ident[:])
                        op.then_inc(pt_full, 1)

                def attend(u):
                    kv, b = u // 2, u % 2
                    bank = open_slot(f"O{u}")
                    if u == 0:
                        pe.wait_ge(ring_free, ring.done("V3"))
                    for t in range(2):
                        pe.wait_ge(pt_low, i * (2 * UNITS) + (2 * u + t + 1))
                        block_ = b if t == 0 else 2 + b
                        for n, (pa, pb) in enumerate(PASSES):
                            op = nc.tensor.matmul(bank[0:HD], v_sb[:, pa, block_, kv * HD:(kv + 1) * HD], pT[:, pb, t],
                                                  start=(t == 0 and n == 0), stop=(t == 1 and n == len(PASSES) - 1))
                    op.then_inc(ring_full, 1)

                def project_out(b, kvs):
                    for kv in kvs:
                        pe.wait_ge(ring_free, ring.done(f"O{2 * kv + b}"))
                        for j in range(QT):
                            t = kv * QT + j
                            op = nc.tensor.matmul(ps_scores[:, b, 0:D], oT[:, t, b * TOK:(b + 1) * TOK], woT[:, t],
                                                  start=(t == 0), stop=(t == KV * QT - 1), skip_group_check=True)
                    if kv == KV - 1:
                        op.then_inc(y_full, 1)

                for job in ("K0", "K1", "K2", "Q0.0", "Q0.1", "Q0.2"):
                    project(job)
                scores(0)
                scores(1)
                for job in ("V0", "V1", "V2", "V3", "Q1.0", "Q1.1", "Q1.2"):
                    project(job)
                for u in range(UNITS):
                    transpose_probs(u)
                    if u + 2 < UNITS:
                        scores(u + 2)
                    for job in SPREAD.get(u, ()):
                        if not (last and job[0] == "H"):
                            project(job)
                    if u >= UNITS - 2:
                        project_out(u % 2, range(KV - 1))
                    attend(u)
                project_out(0, [KV - 1])
                project_out(1, [KV - 1])

            with pe.Fori(0, PAIRS - 1, 1) as i:
                body(i, False)
            body(PAIRS - 1, True)

            pe.wait_ge(y_free, 2 * PAIRS)
            for m in range(BATCH):
                pe.wait_ge(f_ln, m + 1)
                if m >= 4:
                    pe.wait_ge(xt_low, m - 3)
                bank = ps_pt[:, m % 4] if m % 4 < 2 else ps_ring[:, m % 4 - 2]
                for c in range(DC):
                    op = nc.tensor.transpose(bank[:, c * P:(c + 1) * P], x1t[:, m % 2, c * P:(c + 1) * P], ident[:])
                op.then_inc(xt_full, 1)

            def down_tile(hf, n):
                w, at = (P if n < NT - 1 else LAST_N), hf * NT + n
                pe.wait_ge(h_low, at + 1)
                if n == 0:
                    if hf == 0:
                        pe.wait_ge(xt_low, BATCH)
                    else:
                        pe.wait_ge(f_y_free, 4)
                for m in range(4):
                    bank = ps_pt[:, m] if m < 2 else ps_ring[:, m - 2]
                    for k, (a, b) in enumerate(PASSES):
                        op = nc.tensor.matmul(bank, hidden[0:w, at % 2, a, m * P:(m + 1) * P], wd[0:w, b, n],
                                              start=(n == 0 and k == 0), stop=(n == NT - 1 and k == len(PASSES) - 1))
                    if n == NT - 1:
                        op.then_inc(f_y_full, 1)
                if n < NT - 1:
                    op.then_inc(down_done, 1)

            for hf in range(2):
                tokens = slice(hf * 512, (hf + 1) * 512)
                for n in range(NT):
                    w, at = (P if n < NT - 1 else LAST_N), hf * NT + n
                    if hf == 0:
                        pe.wait_ge(w_low, n + 1)
                    if n == 0:
                        pe.wait_ge(xt_low, 4 * (hf + 1))
                    for mat, full, cols in ((0, g_full, 0), (1, u_full, 512)):
                        if at >= 2:
                            pe.wait_ge(silu_done if mat == 0 else h_done, at - 1)
                        for c in range(DC):
                            for k, (a, b) in enumerate(PASSES):
                                op = nc.tensor.matmul(ps_scores[0:w, at % 2, cols:cols + 512],
                                                      wgu[:, a, mat, c, n * P:n * P + w], x2T[:, b, c, tokens],
                                                      start=(c == 0 and k == 0), stop=(c == DC - 1 and k == len(PASSES) - 1))
                        op.then_inc(full, 1)
                    if n > 0:
                        down_tile(hf, n - 1)
                down_tile(hf, NT - 1)


_INS = ["x", "ctx_4096", "g_xattn", "g_ffn", "L0_xattn_Wq", "L0_xattn_Wk", "L0_xattn_Wv", "L0_xattn_Wo"] + [
    f"L0_ffn_{m}_{w}" for m in ("gate", "up", "down") for w in ("qweight", "scales", "qzeros", "g_idx")]


def kernel(**inputs):
    import numpy as _np
    import concourse.bacc as _bacc
    from concourse import mybir as _mybir
    from concourse.bass_utils import run_bass_kernel_spmd as _run

    nc = _bacc.Bacc("TRN2", target_bir_lowering=False, num_devices=1)
    arrays, args = {}, []
    for name in _INS:
        a = _np.ascontiguousarray(inputs[name])
        arrays[f"in_{name}_dram"] = a
        args.append(nc.dram_tensor(f"in_{name}_dram", a.shape, _mybir.dt.from_np(a.dtype), kind="ExternalInput").ap())
    out = nc.dram_tensor("out_0_dram", (BATCH, TOK, D), F32, kind="ExternalOutput").ap()
    build(nc, *args[:8], args[8:12], args[12:16], args[16:20], out)
    r = _run(nc, [arrays], core_ids=[0])
    return r.results[0]["out_0_dram"]
```

```python
from contextlib import ExitStack

import concourse.bass as bass
from concourse import mybir

F32 = mybir.dt.float32
F32R = mybir.dt.float32r
I32 = mybir.dt.int32
ALU = mybir.AluOpType
ACT = mybir.ActivationFunctionType
AX = mybir.AxisListType

P = 128
BATCH, TOK, D = 8, 128, 512
HEADS, KV, HD = 16, 4, 96
GROUP = HEADS // KV
DC = D // P
PAIRS = BATCH // 2
QT = 3
TAIL = 32
INTER = 1376
NT = (INTER + P - 1) // P
LAST_N = INTER - (NT - 1) * P
SCALE = float(HD) ** -0.5
EPS = 1e-5
HIGH, LOW = 0, 1
PASSES = ((HIGH, HIGH), (HIGH, LOW), (LOW, HIGH))

PACK = 8
ZB = 2
NB = INTER // ZB
GATE_GROUPS, DOWN_GROUPS = D // P, INTER // P

UNITS = 2 * KV
NEXT_HEAD = "H0 H1 H2 H3"
NEXT_Q0 = "Q0.0 Q0.1 Q0.2"
NEXT_K = "K0 K1 K2"
PRO_STEPS = f"{NEXT_HEAD} {NEXT_Q0} {NEXT_K} S8 Q1.0 Q1.1 R8 Q1.2 S9".split()


PAIR_STEPS = """
    V0 V1 R1 V2 V3
    P0 Q2.0 S2 O0 D0 Q2.1 R2
    P1 Q2.2 S3 O1 D1 Y0 R3 L
    P2 Q3.0 Q3.1 S4 O2 D2 Y1 R4 A
    P3 Q3.2 H0 S5 O3 D3 Y2 H1 R5
    P4 H2 H3 S6 O4 D4 Y3 R6
    P5 Q0.0 Q0.1 S7 O5 D5 Y4 R7
    P6 Q0.2 O6 K0 D6 Y5 K1
    K2 P7 O7 Y6 Q1.0 Q1.1 S8 Y7 R8 Q1.2 S9""".split()
LAST_STEPS = """
    V0 V1 R1 V2 V3
    P0 Q2.0 S2 O0 D0 Q2.1 R2
    P1 Q2.2 S3 O1 D1 Y0 R3 N0
    P2 Q3.0 Q3.1 S4 O2 D2 Y1 R4 N1
    P3 Q3.2 S5 O3 D3 Y2 R5 N2
    P4 S6 O4 D4 Y3 R6 T0
    P5 S7 O5 D5 Y4 R7 T1 W0
    P6 X0 X1 O6 Y5 X2 T2
    P7 X3 O7 W1 Y6 X4 X5 Y7""".split()
EARLY = 6
W_EARLY = 2


def pair_steps(last):
    return LAST_STEPS if last else PAIR_STEPS


def ring_jobs(steps):
    return [s for s in steps if s[0] in "VQHKOYX"]


W_SPLIT = 2 * QT + HEADS * HD // P
W_JOBS = W_SPLIT + HEADS * HD // P
PRO_JOBS = W_JOBS + len(ring_jobs(PRO_STEPS))
PRO_SPLIT = W_SPLIT + len(ring_jobs(PRO_STEPS))
PAIR_JOBS = len(ring_jobs(pair_steps(False)))
PAIR_SPLIT = PAIR_JOBS - 2 * UNITS
ATT_BANK = len(ring_jobs(LAST_STEPS)) % 2
ATT_SPLIT = PRO_SPLIT + (PAIRS - 1) * PAIR_SPLIT + len(ring_jobs(LAST_STEPS)) - 2 * UNITS
ATT_JOBS = PRO_JOBS + (PAIRS - 1) * PAIR_JOBS + len(ring_jobs(pair_steps(True)))


class Ring:

    def __init__(self, i, steps):
        self.jobs = ring_jobs(steps)
        self.split = [j for j in self.jobs if j[0] not in "OY"]
        self.steps = steps
        if isinstance(i, int) and i < 0:
            self.first, self.first_split = W_JOBS, W_SPLIT
            self.before = self.first - 1
        else:
            self.first, self.first_split = i * PAIR_JOBS + PRO_JOBS, i * PAIR_SPLIT + PRO_SPLIT
            self.before = self.first

    def bank(self, job):
        return self.jobs.index(job) % 2

    def done(self, job):
        return self.first + (self.jobs.index(job) + 1)

    def slot(self, job):
        n = self.jobs.index(job)
        return self.first + (n - 1) if n else self.before

    def high(self, job):
        return self.first_split + (self.split.index(job) + 1)


def dequant_blocks(i, last):
    out = [("gate", 0, i, P), ("gate", 1, i, P), ("up", 0, i, P), ("up", 1, i, P)]
    for k in range(3):
        if last and 3 * i + k >= NT:
            continue
        rows = LAST_N if last and 3 * i + k == NT - 1 else P
        out.append(("down", 0, i * 3 + k, rows))
    return out


BLOCKS_PER_PAIR = 7
ZROWS = GATE_GROUPS * ZB
ZTAB = 2 * ZROWS + DOWN_GROUPS


def build(nc, x, ctx, g_xattn, g_ffn, Wq, Wk, Wv, Wo, gate, up, down, out):
    quant = {"gate": gate, "up": up, "down": down}
    with ExitStack() as top:
        def sem(name):
            return top.enter_context(nc.semaphore(name))

        def sbuf(stack, name, shape, dt=F32):
            return stack.enter_context(nc.sbuf_tensor(name, shape, dt))

        x1_scratch = nc.dram_tensor("x1_scratch", (BATCH, TOK, D), F32, kind="Internal").ap()
        wgu_scratch = nc.dram_tensor("wgu_scratch", (2, DC, P, INTER), F32, kind="Internal").ap()
        wd_scratch = nc.dram_tensor("wd_scratch", (NT * P, D), F32, kind="Internal").ap()
        table_gu = nc.dram_tensor("table_gu", (2, GATE_GROUPS * ZB, 2, NB), F32, kind="Internal").ap()
        table_d = nc.dram_tensor("table_d", (DOWN_GROUPS, 2, D), F32, kind="Internal").ap()

        ps_scores = top.enter_context(nc.psum_tensor("ps_scores", [P, 2, GROUP * 256], F32))
        ps_pt = top.enter_context(nc.psum_tensor("ps_pt", [P, 2, 512], F32))
        ps_ring = top.enter_context(nc.psum_tensor("ps_ring", [P, 2, 512], F32))

        ident = sbuf(top, "ident", [P, P])
        gates = sbuf(top, "gates", [P, 2])
        tgate = sbuf(top, "tgate", [P, 2])
        neg_half = sbuf(top, "neg_half", [P, BATCH])
        bn = sbuf(top, "bn", [P, BATCH, 6])
        mv = sbuf(top, "mv", [P, BATCH, 2])
        veps = sbuf(top, "veps", [P, BATCH])
        rstd = sbuf(top, "rstd", [P, BATCH])
        xres = sbuf(top, "xres", [P, 2, D])

        att = ExitStack()
        wqT = sbuf(att, "wqT", [P, 2, DC, HEADS * HD], F32R)
        wkT = sbuf(att, "wkT", [P, 2, DC, KV * HD], F32R)
        wvT = sbuf(att, "wvT", [P, 2, DC, KV * HD], F32R)
        hT = sbuf(att, "hT", [P, 2, DC, 4, P], F32R)
        xin = sbuf(att, "xin", [P, 4, D])
        with ExitStack() as raw:
            wq_raw = sbuf(raw, "wq_raw", [P, KV * QT, D])
            wk_raw = sbuf(raw, "wk_raw", [P, QT, D])
            wv_raw = sbuf(raw, "wv_raw", [P, QT, D])
            wo_raw = sbuf(raw, "wo_raw", [P, DC, KV * QT, P])
        kT = sbuf(att, "kT", [P, 2, QT, 512], F32R)
        k3T = sbuf(att, "k3T", [P, 2, 512], F32R)
        qT = [sbuf(att, f"qT{n}", [P, 2, QT, 2 * TOK], F32R) for n in range(2)]
        q3T = [sbuf(att, f"q3T{n}", [P, 2, 2 * TOK], F32R) for n in range(2)]
        v_sb = sbuf(att, "v_sb", [P, 2, 4, KV * HD], F32R)
        probs = sbuf(att, "probs", [P, 2, GROUP, 256])
        pT = sbuf(att, "pT", [P, 2, 2, 512], F32R)
        woT = sbuf(att, "woT", [P, KV * QT, D])
        oT = sbuf(att, "oT", [P, 2, QT, TOK])
        dq_t = sbuf(att, "dq_t", [P, 2, 2 * NB])
        dq_q = sbuf(att, "dq_q", [P, 2, NB], I32)
        gidx_i = sbuf(att, "gidx_i", [P, 2 * DC + NT], I32)
        gidx = sbuf(att, "gidx", [P, 2 * DC + NT])
        gneg = sbuf(att, "gneg", [P, 2 * DC + NT])
        idx = sbuf(att, "idx", [P, 2], I32)
        shift_row = sbuf(att, "shift_row", [P, 1], I32)
        shift_col = sbuf(att, "shift_col", [P, PACK], I32)
        rowno = sbuf(att, "rowno", [P, 1], I32)
        negmax = sbuf(att, "negmax", [P, 2, GROUP])
        sums = sbuf(att, "sums", [P, 2, GROUP])
        rsums = sbuf(att, "rsums", [P, 2, GROUP])
        att.close()

        with ExitStack() as early:
            sbuf(early, "room_of_wqT", [P, 2, DC, HEADS * HD])
            x1n = sbuf(early, "x1n", [P, EARLY, D])
        ffn = ExitStack()
        wgu = sbuf(ffn, "wgu", [P, NT, 2, 2, DC, P], F32R)
        st_gu = sbuf(ffn, "st_gu", [P, 2, 2, DC, P])
        x2T = sbuf(ffn, "x2T", [P, 2, DC, BATCH * TOK], F32R)
        wd = sbuf(ffn, "wd", [P, NT, 2, D], F32R)
        hidden = sbuf(ffn, "hidden", [P, 2, 2, 512], F32R)
        silu = sbuf(ffn, "silu", [P, 2, 512])
        res = sbuf(ffn, "res", [P, 4, D])
        st_d = sbuf(ffn, "st_d", [P, 2, D])
        ffn.close()

        const_ready = sem("const_ready")
        shifts_ready = sem("shifts_ready")
        wk_in, wv_in, wo_in = sem("wk_in"), sem("wv_in"), sem("wo_in")
        wq_in = sem("wq_in")
        small_in = sem("small_in")
        x_in = sem("x_in")
        ln_stat = sem("ln_stat")
        ln_var = sem("ln_var")
        ln_rstd = sem("ln_rstd")
        ln_done = sem("ln_done")
        tanh_done = sem("tanh_done")
        ring_full, ring_high, ring_free = sem("ring_full"), sem("ring_high"), sem("ring_free")
        s_full, maxed, expd, recip, normed = (sem(n) for n in ("s_full", "maxed", "expd", "recip", "normed"))
        pt_full, pt_high, pt_low = sem("pt_full"), sem("pt_high"), sem("pt_low")
        xres_in, x1_out = sem("xres_in"), sem("x1_out")
        gi_chain = sem("gi_chain")
        zraw_clear, zraw_in, table_out, z_chain = (sem(n) for n in ("zraw_clear", "zraw_in", "table_out", "z_chain"))
        gathered, q_in = [sem("gathered0"), sem("gathered1")], [sem("q_in0"), sem("q_in1")]
        idx_ready, unpacked, w_ready, w_out, dq_chain = (
            sem(n) for n in ("idx_ready", "unpacked", "w_ready", "w_out", "dq_chain"))
        stage_in = [sem("stage_in0"), sem("stage_in1")]
        stage_d_in = [sem("stage_d_in0"), sem("stage_d_in1")]
        gu_high, gu_low, d_high, d_low = (sem(n) for n in ("gu_high", "gu_low", "d_high", "d_low"))
        passed_v, passed_p = sem("passed_v"), sem("passed_p")
        x1_in = sem("x1_in")
        f_stat, f_mv, f_var, f_rstd, f_ln = (sem(n) for n in ("f_stat", "f_mv", "f_var", "f_rstd", "f_ln"))
        g_full, u_full, silu_done, h_done, h_high, h_low, down_done = (
            sem(n) for n in ("g_full", "u_full", "silu_done", "h_done", "h_high", "h_low", "down_done"))
        f_y_full, f_y_free = sem("f_y_full"), sem("f_y_free")
        res_in, o_out = sem("res_in"), sem("o_out")

        block = top.enter_context(nc.Block())

        def in_rows(src, i):
            return src[bass.ds(i * 2, 2)].rearrange("b p d -> p b d")

        @block.sync
        def _(sp):
            sp.dma_start(xin[:, 0:2, :], in_rows(x, 0)).then_inc(x_in, 16)
            sp.dma_start(xin[:, 2:4, :], in_rows(ctx, 0)).then_inc(x_in, 16)
            sp.dma_start(wk_raw[0:HD], Wk[0:QT * HD].rearrange("(j p) d -> p j d", p=HD)).then_inc(wk_in, 16)
            sp.dma_start(wk_raw[HD:P], Wk[QT * HD:].rearrange("(j p) d -> p j d", p=TAIL)).then_inc(wk_in, 16)
            sp.dma_start(wv_raw[:], Wv.rearrange("(j p) d -> p j d", p=P)).then_inc(wv_in, 16)
            for kv in range(KV):
                rows, dst = Wq[kv * GROUP * HD:(kv + 1) * GROUP * HD], wq_raw[:, kv * QT:(kv + 1) * QT]
                sp.dma_start(dst[0:HD], rows[0:QT * HD].rearrange("(j p) d -> p j d", p=HD)).then_inc(wq_in, 16)
                sp.dma_start(dst[HD:P], rows[QT * HD:].rearrange("(j p) d -> p j d", p=TAIL)).then_inc(wq_in, 16)
            for b in range(DC):
                cols = Wo[b * P:(b + 1) * P].rearrange("p (k c) -> p k c", k=KV)
                dst = wo_raw[:, b].rearrange("p (k j) e -> p k j e", k=KV)
                for kv in range(KV):
                    sp.dma_start(dst[:, kv, :, 0:HD], cols[:, kv, 0:QT * HD].rearrange("p (j e) -> p j e", j=QT)).then_inc(wo_in, 16)
                    sp.dma_start(dst[:, kv, :, HD:P], cols[:, kv, QT * HD:].rearrange("p (j e) -> p j e", j=QT)).then_inc(wo_in, 16)

            sp.dma_start(xres[:], in_rows(x, 0)).then_inc(xres_in, 16)

            sp.wait_ge(zraw_clear, 1)
            for m, name in enumerate(("gate", "up")):
                sp.dma_start(dq_q[m * ZROWS:(m + 1) * ZROWS, 0, 0:NB // PACK],
                             quant[name][2].rearrange("g (b n) -> (g b) n", b=ZB)).then_inc(zraw_in, 16)
                sp.dma_start(table_gu[m, :, 0, :], quant[name][1].rearrange("g (b n) -> (g b) n", b=ZB)).then_inc(table_out, 16)
            sp.dma_start(dq_q[2 * ZROWS:2 * ZROWS + DOWN_GROUPS, 0, 0:D // PACK], down[2]).then_inc(zraw_in, 16)
            sp.dma_start(table_d[:, 0, :], down[1]).then_inc(table_out, 16)
            sp.wait_ge(z_chain, 2)
            zeros = dq_t[:, 1]
            for m in range(2):
                sp.dma_start(table_gu[m, :, 1, :], zeros[m * ZROWS:(m + 1) * ZROWS, 0:NB]).then_inc(table_out, 16)
            sp.dma_start(table_d[:, 1, :], zeros[2 * ZROWS:2 * ZROWS + DOWN_GROUPS, 0:D]).then_inc(table_out, 16)

            def raw_block(i, last, k):
                name, cb, t, rows = dequant_blocks(i, last)[k]
                qw = quant[name][0]
                width, cols = (NB, INTER) if name != "down" else (D, D)
                if k >= 2:
                    sp.wait_ge(w_out, i * (BLOCKS_PER_PAIR * 16) + (k - 1) * 16)
                src = bass.AP(qw.tensor, t * (P // PACK * cols) + cb * NB, [[cols, rows // PACK], [0, PACK], [1, width]])
                sp.dma_start(dq_q[0:rows, k % 2, 0:width], src).then_inc(q_in[k % 2], 16)

            def store_block(i, last, k):
                name, cb, t, rows = dequant_blocks(i, last)[k]
                sp.wait_ge(w_ready, i * BLOCKS_PER_PAIR + (k + 1))
                if name == "down":
                    dst = wd_scratch[bass.ds(t * P, rows)]
                    sp.dma_start(dst, dq_q[0:rows, k % 2, 0:D].bitcast(F32)).then_inc(w_out, 16)
                else:
                    dst = wgu_scratch[("gate", "up").index(name)].rearrange("c p n -> (c p) n")
                    sp.dma_start(dst[bass.ds(t * P, P), cb * NB:(cb + 1) * NB], dq_q[:, k % 2].bitcast(F32)).then_inc(w_out, 16)

            def load_gu(n):
                w = P if n < NT - 1 else LAST_N
                if n >= 2:
                    sp.wait_ge(gu_low, n - 1)
                for m in range(2):
                    src = wgu_scratch[m, :, :, n * P:n * P + w].rearrange("c p n -> p c n")
                    sp.dma_start(st_gu[:, n % 2, m, :, 0:w], src).then_inc(stage_in[n % 2], 16)

            def load_d(n):
                w = P if n < NT - 1 else LAST_N
                if n >= 2:
                    sp.wait_ge(d_low, n - 1)
                sp.dma_start(st_d[0:w, n % 2], wd_scratch[n * P:n * P + w]).then_inc(stage_d_in[n % 2], 16)

            def body(i, last):
                ring = Ring(i, pair_steps(last))
                blocks = len(dequant_blocks(i, last))
                if last:
                    sp.wait_ge(ring_full, ring.first)
                    sp.dma_start(x1n[:], x1_scratch[0:EARLY].rearrange("m p d -> p m d")).then_inc(x1_in, 16)
                if not last:
                    sp.wait_ge(ring_full, ring.first)
                    sp.dma_start(xin[:, 0:2, :], in_rows(x, i + 1)).then_inc(x_in, 16)
                    sp.dma_start(xin[:, 2:4, :], in_rows(ctx, i + 1)).then_inc(x_in, 16)
                raw_block(i, last, 0)
                raw_block(i, last, 1)
                for k in range(blocks):
                    store_block(i, last, k)
                    if k + 2 < blocks:
                        raw_block(i, last, k + 2)
                    if last and k == 3:
                        load_gu(0)
                        load_gu(1)
                if last:
                    load_gu(2)
                for b in range(2):
                    sp.wait_ge(ring_free, ring.done(f"Y{UNITS - 2 + b}"))
                    sp.dma_start(x1_scratch[bass.ds(i * 2 + b, 1)].rearrange("b p d -> (b p) d"), xres[:, b]).then_inc(x1_out, 16)
                if not last:
                    sp.wait_ge(w_out, i * (BLOCKS_PER_PAIR * 16) + BLOCKS_PER_PAIR * 16)
                    sp.wait_ge(x1_out, i * 32 + 32)
                    sp.dma_start(xres[:], in_rows(x, i + 1)).then_inc(xres_in, 16)

            with sp.Fori(0, PAIRS - 1, 1) as i:
                body(i, False)
            body(PAIRS - 1, True)

            sp.wait_ge(x1_out, PAIRS * 32)
            sp.wait_ge(w_out, 16 * (BLOCKS_PER_PAIR * PAIRS - 1))
            sp.wait_ge(ring_free, ATT_JOBS)
            load_d(0)
            load_d(1)

            def load_res(hf):
                sp.dma_start(res[:], x1_scratch[hf * 4:hf * 4 + 4].rearrange("m p d -> p m d")).then_inc(res_in, 16)

            load_res(0)
            for n in range(3, NT):
                load_gu(n)
                load_d(n - 1)
            load_d(NT - 1)
            for hf in range(2):
                if hf == 1:
                    sp.wait_ge(o_out, 64)
                    load_res(1)
                for m in range(4):
                    sp.wait_ge(f_y_free, hf * 4 + m + 1)
                    sp.dma_start(out[hf * 4 + m], res[:, m]).then_inc(o_out, 16)
            sp.wait_ge(o_out, 16 * BATCH)

        @block.gpsimd
        def _(pool):
            nc.gpsimd.memset(ident[:], 0.0).then_inc(const_ready, 1)
            pool.wait_ge(const_ready, 1)
            nc.gpsimd.affine_select(out=ident[:], in_=ident[:], compare_op=ALU.not_equal, fill=1.0, base=0,
                                    pattern=[[-1, P]], channel_multiplier=1).then_inc(const_ready, 1)
            nc.gpsimd.memset(neg_half[:], -0.5).then_inc(const_ready, 1)
            nc.gpsimd.iota(rowno[:], pattern=[[0, 1]], base=0, channel_multiplier=1).then_inc(const_ready, 1)
            nc.gpsimd.iota(shift_col[:], pattern=[[4, PACK]], base=0, channel_multiplier=0).then_inc(const_ready, 1)

            def ln_power(n):
                pool.wait_ge(ln_var, n)
                nc.gpsimd.tensor_tensor(out=rstd[:, 0:2], in0=veps[:, 0:2], in1=neg_half[:, 0:2], op=ALU.pow).then_inc(ln_rstd, 1)

            def ffn_power(k):
                pool.wait_ge(f_var, k + 1)
                cols = slice(2 * k, 2 * k + 2)
                nc.gpsimd.tensor_tensor(out=rstd[:, cols], in0=veps[:, cols], in1=neg_half[:, cols], op=ALU.pow).then_inc(f_rstd, 1)

            def carry():
                pool.sem_inc(passed_p, 1)

            def normalise(i, u):
                pool.wait_ge(recip, i * UNITS + (u + 1))
                carry()
                for h in range(GROUP):
                    op = nc.gpsimd.tensor_scalar(probs[:, u % 2, h], probs[:, u % 2, h], rsums[:, u % 2, h:h + 1], 1.0,
                                                 ALU.mult, ALU.mult)
                op.then_inc(normed, 1)

            def gather(i, last, k):
                name, cb, t, rows = dequant_blocks(i, last)[k]
                width = NB if name != "down" else D
                table = table_d if name == "down" else table_gu.rearrange("m g t n -> (m g) t n")
                pool.wait_ge(idx_ready, i * BLOCKS_PER_PAIR + (k + 1))
                if k >= 2:
                    pool.wait_ge(w_ready, i * BLOCKS_PER_PAIR + (k - 1))
                carry()
                at = bass.IndirectOffsetOnAxis(ap=idx[0:rows, k % 2:k % 2 + 1], axis=0)
                nc.gpsimd.indirect_dma_start(dq_t[0:rows, k % 2, 0:2 * width], None, table.rearrange("g t n -> g (t n)"), at).then_inc(gathered[k % 2], 16)

            def rescale(i, last, k):
                name, cb, t, rows = dequant_blocks(i, last)[k]
                width = NB if name != "down" else D
                pool.wait_ge(unpacked, i * BLOCKS_PER_PAIR + (k + 1))
                w = dq_q[0:rows, k % 2, 0:width].bitcast(F32)
                nc.gpsimd.tensor_tensor(out=w, in0=w, in1=dq_t[0:rows, k % 2, 0:width], op=ALU.mult).then_inc(w_ready, 1)

            pool.wait_ge(const_ready, 3)
            ln_power(1)

            pool.wait_ge(table_out, 16 * 6)

            def follow(i, last, steps):
                blocks = len(dequant_blocks(i, last))
                for step in steps:
                    n = int(step[1]) if step[1:] else 0
                    if step[0] == "R":
                        normalise(i, n)
                    elif step[0] == "D" and n < blocks:
                        if n + 1 < blocks:
                            gather(i, last, n + 1)
                        rescale(i, last, n)
                    elif step == "L":
                        ln_power(i + 2)
                    elif step[0] == "N":
                        ffn_power(n)

            def body(i, last):
                gather(i, last, 0)
                follow(i, last, pair_steps(last))
                if not last:
                    pool.wait_ge(w_ready, i * BLOCKS_PER_PAIR + BLOCKS_PER_PAIR)

            follow(-1, False, PRO_STEPS)
            with pool.Fori(0, PAIRS - 1, 1) as i:
                body(i, False)
            body(PAIRS - 1, True)
            ffn_power(BATCH // 2 - 1)

        @block.scalar
        def _(act):
            act.dma_start(gates[:, 0:1], bass.AP(g_xattn.tensor, 0, [[0, P], [1, 1]])).then_inc(small_in, 16)
            act.dma_start(gates[:, 1:2], bass.AP(g_ffn.tensor, 0, [[0, P], [1, 1]])).then_inc(small_in, 16)
            act.wait_ge(gi_chain, 1)
            act.dma_start(gidx_i[:, 0:DC], gate[3].rearrange("(c p) -> p c", p=P), allow_slow_non_contiguous=True).then_inc(small_in, 16)
            act.dma_start(gidx_i[:, DC:2 * DC], up[3].rearrange("(c p) -> p c", p=P), allow_slow_non_contiguous=True).then_inc(small_in, 16)
            act.dma_start(gidx_i[:, 2 * DC:2 * DC + NT - 1],
                           down[3][0:(NT - 1) * P].rearrange("(c p) -> p c", p=P), allow_slow_non_contiguous=True).then_inc(small_in, 16)
            act.dma_start(gidx_i[0:LAST_N, 2 * DC + NT - 1:], down[3][(NT - 1) * P:].rearrange("(c p) -> p c", c=1), allow_slow_non_contiguous=True).then_inc(small_in, 16)
            act.wait_ge(small_in, 96)
            nc.scalar.activation(tgate[:], gates[:], ACT.Tanh).then_inc(tanh_done, 1)

            def high(job_done, bank, dst, cols=512, shape=None, scale=1.0):
                act.wait_ge(ring_full, job_done)
                src = ps_ring[:, bank, 0:cols]
                if shape:
                    src = src.rearrange(*shape[0], **shape[1])
                if isinstance(dst, list):
                    nc.scalar.activation(dst[1], src[HD:P], ACT.Copy, scale=scale)
                    dst, src = dst[0], src[0:HD]
                nc.scalar.activation(dst, src, ACT.Copy, scale=scale).then_inc(ring_high, 1)

            by_chunk = (("p (c n) -> p c n",), {"c": DC})
            for job in range(2 * QT + HEADS * HD // P):
                dst, t = (wkT, job) if job < QT else (wvT, job - QT) if job < 2 * QT else (wqT, job - 2 * QT)
                high(job + 1, job % 2, dst[:, HIGH, :, t * P:(t + 1) * P], shape=by_chunk)
            def x_high(m, done, bank):
                high(done, bank, x2T[:, HIGH, :, m * P:(m + 1) * P], shape=by_chunk)

            def split_gu(n):
                w = P if n < NT - 1 else LAST_N
                act.wait_ge(stage_in[n % 2], 32 * (n // 2 + 1))
                nc.scalar.activation(wgu[:, n, HIGH, :, :, 0:w], st_gu[:, n % 2, :, :, 0:w], ACT.Copy).then_inc(gu_high, 1)

            def follow(i, steps):
                ring = Ring(i, steps)

                def evacuate(job):
                    done, bank = ring.done(job), ring.bank(job)
                    if job[0] == "K":
                        j = int(job[1])
                        high(done, bank, [kT[0:HD, HIGH, j].rearrange("p (b t s) -> p t b s", b=2, t=2),
                                          k3T[TAIL * j:TAIL * (j + 1), HIGH].rearrange("p (b t s) -> p t b s", b=2, t=2)],
                             shape=(("p (t b s) -> p t b s",), {"b": 2, "t": 2}))
                    elif job[0] == "V":
                        high(done, bank, v_sb[:, HIGH, int(job[1])], KV * HD)
                    elif job[0] == "Q":
                        g, j = int(job[1]) % 2, int(job[3])
                        high(done, bank, [qT[g][0:HD, HIGH, j], q3T[g][TAIL * j:TAIL * (j + 1), HIGH]], 2 * TOK, scale=SCALE)
                    elif job[0] == "X":
                        x_high(int(job[1]), done, bank)
                    else:
                        high(done, bank, hT[:, HIGH, :, int(job[1]), :], shape=by_chunk)

                def exponentials(u):
                    act.wait_ge(maxed, i * UNITS + (u + 1))
                    for h in range(GROUP):
                        op = nc.scalar.activation(probs[:, u % 2, h], ps_scores[:, u % 2, h * 256:(h + 1) * 256], ACT.Exp,
                                                  bias=negmax[:, u % 2, h:h + 1], accum_out=sums[:, u % 2, h:h + 1])
                    op.then_inc(expd, 1)

                for step in steps:
                    if step in ring.split:
                        evacuate(step)
                    elif step[0] == "S":
                        exponentials(int(step[1]))
                    elif step[0] == "W":
                        split_gu(int(step[1]))
                    elif step[0] == "P":
                        for t in range(2):
                            act.wait_ge(pt_full, i * (2 * UNITS) + (2 * int(step[1]) + t + 1))
                            nc.scalar.activation(pT[:, HIGH, t], ps_pt[:, t], ACT.Copy).then_inc(pt_high, 1)

            def body(i, last):
                follow(i, pair_steps(last))

            follow(-1, PRO_STEPS)
            with act.Fori(0, PAIRS - 1, 1) as i:
                body(i, False)
            body(PAIRS - 1, True)

            act.wait_ge(ring_free, ATT_JOBS)
            act.wait_ge(w_ready, BLOCKS_PER_PAIR * PAIRS - 1)

            def split_d(n):
                w = P if n < NT - 1 else LAST_N
                act.wait_ge(stage_d_in[n % 2], 16 * (n // 2 + 1))
                nc.scalar.activation(wd[0:w, n, HIGH], st_d[0:w, n % 2], ACT.Copy).then_inc(d_high, 1)

            for hf in range(2):
                for n in range(NT):
                    w, at = (P if n < NT - 1 else LAST_N), hf * NT + n
                    act.wait_ge(g_full, at + 1)
                    if at >= 2:
                        act.wait_ge(h_low, at - 1)
                    nc.scalar.activation(silu[0:w, at % 2], ps_scores[0:w, at % 2, 0:512], ACT.Silu).then_inc(silu_done, 1)
                    if hf == 0:
                        if n == 0:
                            for m in range(EARLY, BATCH):
                                x_high(m, ATT_JOBS + m - EARLY + 1, (ATT_BANK + m - EARLY) % 2)
                        split_d(n)
                    act.wait_ge(h_done, at + 1)
                    if at >= 2:
                        act.wait_ge(down_done, at - 1)
                    nc.scalar.activation(hidden[0:w, at % 2, HIGH], silu[0:w, at % 2], ACT.Copy).then_inc(h_high, 1)
                    if hf == 0 and n + W_EARLY < NT:
                        split_gu(n + W_EARLY)

        @block.vector
        def _(dve):
            nc.vector.memset(gidx_i[:], 0).then_inc(gi_chain, 1)
            nc.vector.memset(dq_q[:, 0, 0:NB // PACK], 0).then_inc(zraw_clear, 1)

            def layer_norm(i_next, wait_in):
                dve.wait_ge(x_in, wait_in)
                for m in range(2):
                    nc.vector.bn_stats(bn[:, m], xin[:, m]).then_inc(ln_stat, 1)
                base = i_next * 4
                dve.wait_ge(ln_stat, base + 2)
                dve.sem_inc(passed_v, 1)
                for m in range(2):
                    nc.vector.bn_aggr(mv[:, m], bn[:, m]).then_inc(ln_stat, 1)
                dve.wait_ge(ln_stat, base + 4)
                nc.vector.tensor_scalar(veps[:, 0:2], mv[:, 0:2, 1], EPS, None, ALU.add).then_inc(ln_var, 1)

            def layer_norm_apply(i_next):
                dve.wait_ge(ln_rstd, i_next + 1)
                for m in range(2):
                    op = nc.vector.tensor_scalar(xin[:, m], xin[:, m], mv[:, m, 0:1], rstd[:, m:m + 1], ALU.subtract, ALU.mult)
                op.then_inc(ln_done, 1)

            def low(high_done, bank, dst, hi, cols=512, shape=None, scale=None):
                dve.wait_ge(ring_high, high_done)
                src = ps_ring[:, bank, 0:cols]
                if shape:
                    src = src.rearrange(*shape[0], **shape[1])

                def rest(dst, src, hi):
                    if scale is None:
                        return nc.vector.tensor_tensor(dst, src, hi.bitcast(F32), ALU.subtract)
                    return nc.vector.scalar_tensor_tensor(out=dst, in0=src, scalar=scale, in1=hi.bitcast(F32), op0=ALU.mult,
                                                          op1=ALU.subtract)

                if isinstance(dst, list):
                    rest(dst[1], src[HD:P], hi[1])
                    dst, hi, src = dst[0], hi[0], src[0:HD]
                rest(dst, src, hi).then_inc(ring_free, 1)

            dve.wait_ge(const_ready, 5)
            nc.vector.tensor_scalar(shift_row[:], rowno[:], PACK - 1, 2, ALU.bitwise_and, ALU.logical_shift_left).then_inc(shifts_ready, 1)
            by_chunk = (("p (c n) -> p c n",), {"c": DC})
            layer_norm(0, 32)
            for job in range(2 * QT + HEADS * HD // P):
                dst, t = (wkT, job) if job < QT else (wvT, job - QT) if job < 2 * QT else (wqT, job - 2 * QT)
                low(job + 1, job % 2, dst[:, LOW, :, t * P:(t + 1) * P], dst[:, HIGH, :, t * P:(t + 1) * P], shape=by_chunk)
                if job == 2:
                    layer_norm_apply(0)
            first = 2 * QT + HEADS * HD // P
            for t in range(KV * QT):
                job = first + t
                dve.wait_ge(ring_full, job + 1)
                nc.vector.tensor_copy(woT[:, t], ps_ring[:, job % 2]).then_inc(ring_free, 1)

            dve.wait_ge(small_in, 96)
            nc.vector.tensor_copy(gidx[:], gidx_i[:]).then_inc(gi_chain, 1)
            dve.wait_ge(gi_chain, 2)
            for cols, groups in ((slice(0, 2 * DC), GATE_GROUPS), (slice(2 * DC, 2 * DC + NT), DOWN_GROUPS)):
                nc.vector.tensor_scalar(gneg[:, cols], gidx[:, cols], 0.0, float(groups), ALU.is_lt, ALU.mult).then_inc(gi_chain, 1)
            dve.wait_ge(gi_chain, 4)
            nc.vector.tensor_tensor(gidx[:], gidx[:], gneg[:], ALU.add).then_inc(gi_chain, 1)
            dve.wait_ge(gi_chain, 5)
            for cols, groups in ((slice(0, 2 * DC), GATE_GROUPS), (slice(2 * DC, 2 * DC + NT), DOWN_GROUPS)):
                nc.vector.tensor_scalar(gidx[:, cols], gidx[:, cols], 0.0, float(groups - 1), ALU.max, ALU.min).then_inc(gi_chain, 1)
            dve.wait_ge(gi_chain, 7)
            dve.wait_ge(shifts_ready, 1)
            dve.wait_ge(tanh_done, 1)

            dve.wait_ge(zraw_in, 48)
            zeros = dq_t[0:ZTAB, 1, 0:NB].bitcast(I32)
            nc.vector.tensor_tensor(zeros.rearrange("p (c j) -> p c j", j=PACK),
                                    dq_q[0:ZTAB, 0, 0:NB // PACK].unsqueeze(2).to_broadcast([ZTAB, NB // PACK, PACK]),
                                    shift_col[0:ZTAB].unsqueeze(1).to_broadcast([ZTAB, NB // PACK, PACK]),
                                    ALU.logical_shift_right).then_inc(z_chain, 1)
            dve.wait_ge(z_chain, 1)
            nc.vector.tensor_scalar(zeros, zeros, PACK * 2 - 1, None, ALU.bitwise_and).then_inc(z_chain, 1)

            def indices(i, last, k):
                name, cb, t, rows = dequant_blocks(i, last)[k]
                col = {"gate": 0, "up": DC, "down": 2 * DC}[name] + t
                split = ZB if name != "down" else 1
                cb += ZROWS if name == "up" else 0
                nc.vector.tensor_scalar(idx[:, k % 2:k % 2 + 1], gidx[:, bass.ds(col, 1)], float(split), float(cb), ALU.mult, ALU.add).then_inc(idx_ready, 1)

            def unpack(i, last, k):
                name, cb, t, rows = dequant_blocks(i, last)[k]
                width = NB if name != "down" else D
                n = i * BLOCKS_PER_PAIR + (k + 1)
                transfers = i * (16 * ((BLOCKS_PER_PAIR + 1 - k % 2) // 2)) + 16 * (k // 2 + 1)
                dve.wait_ge(q_in[k % 2], transfers)
                q = dq_q[0:rows, k % 2, 0:width]
                nc.vector.tensor_scalar(q, q, shift_row[0:rows, 0:1], PACK * 2 - 1, ALU.logical_shift_right,
                                        ALU.bitwise_and).then_inc(dq_chain, 1)
                dve.wait_ge(gathered[k % 2], transfers)
                dve.wait_ge(dq_chain, n)
                nc.vector.scalar_tensor_tensor(out=q.bitcast(F32), in0=q, scalar=1.0,
                                               in1=dq_t[0:rows, k % 2, width:2 * width].bitcast(I32), op0=ALU.subtract,
                                               op1=ALU.subtract).then_inc(unpacked, 1)

            def x_low(m, done, bank):
                cols = slice(m * P, (m + 1) * P)
                low(done, bank, x2T[:, LOW, :, cols], x2T[:, HIGH, :, cols], shape=by_chunk)

            def ffn_norm(k, rows):
                for m in range(2):
                    nc.vector.bn_stats(bn[:, 2 * k + m], rows[:, m]).then_inc(f_stat, 1)
                dve.wait_ge(f_stat, 2 * k + 2)
                for m in range(2):
                    nc.vector.bn_aggr(mv[:, 2 * k + m], bn[:, 2 * k + m]).then_inc(f_mv, 1)
                dve.wait_ge(f_mv, 2 * k + 2)
                nc.vector.tensor_scalar(veps[:, 2 * k:2 * k + 2], mv[:, 2 * k:2 * k + 2, 1], EPS, None, ALU.add).then_inc(f_var, 1)

            def ffn_norm_apply(k, rows, dst):
                dve.wait_ge(f_rstd, k + 1)
                for m in range(2):
                    op = nc.vector.tensor_scalar(dst[:, m], rows[:, m], mv[:, 2 * k + m, 0:1], rstd[:, 2 * k + m:2 * k + m + 1],
                                                 ALU.subtract, ALU.mult)
                op.then_inc(f_ln, 1)

            def split_gu(n):
                w = P if n < NT - 1 else LAST_N
                dve.wait_ge(gu_high, n + 1)
                nc.vector.tensor_tensor(wgu[:, n, LOW, :, :, 0:w], st_gu[:, n % 2, :, :, 0:w],
                                        wgu[:, n, HIGH, :, :, 0:w].bitcast(F32), ALU.subtract).then_inc(gu_low, 1)

            def follow(i, last, steps):
                ring = Ring(i, steps)
                blocks = len(dequant_blocks(i, last))

                def evacuate(job):
                    done, bank = ring.high(job), ring.bank(job)
                    if job[0] == "K":
                        j = int(job[1])

                        def dst(part):
                            return [kT[0:HD, part, j].rearrange("p (b t s) -> p t b s", b=2, t=2),
                                    k3T[TAIL * j:TAIL * (j + 1), part].rearrange("p (b t s) -> p t b s", b=2, t=2)]

                        low(done, bank, dst(LOW), dst(HIGH), shape=(("p (t b s) -> p t b s",), {"b": 2, "t": 2}))
                    elif job[0] == "V":
                        low(done, bank, v_sb[:, LOW, int(job[1])], v_sb[:, HIGH, int(job[1])], KV * HD)
                    elif job[0] == "Q":
                        q, j = int(job[1]) % 2, int(job[3])

                        def dst(part):
                            return [qT[q][0:HD, part, j], q3T[q][TAIL * j:TAIL * (j + 1), part]]

                        low(done, bank, dst(LOW), dst(HIGH), 2 * TOK, scale=SCALE)
                    elif job[0] == "X":
                        x_low(int(job[1]), done, bank)
                    else:
                        low(done, bank, hT[:, LOW, :, int(job[1]), :], hT[:, HIGH, :, int(job[1]), :], shape=by_chunk)

                def maxima(u):
                    dve.wait_ge(s_full, i * UNITS + (u + 1))
                    nc.vector.tensor_reduce(negmax[:, u % 2], ps_scores[:, u % 2].rearrange("p (h s) -> p h s", h=GROUP),
                                            AX.X, ALU.max, negate=True).then_inc(maxed, 1)

                def reciprocals(u):
                    dve.wait_ge(expd, i * UNITS + (u + 1))
                    nc.vector.reciprocal(rsums[:, u % 2], sums[:, u % 2]).then_inc(recip, 1)

                def attention_out(u):
                    kv, b = u // 2, u % 2
                    dve.wait_ge(ring_full, ring.done(f"O{u}"))
                    o = ps_ring[0:HD, ring.bank(f"O{u}")].rearrange("p (h q) -> p h q", h=GROUP)
                    tiles = oT[:, b]
                    for j in range(QT):
                        nc.vector.tensor_copy(tiles[HD:P, j], o[TAIL * j:TAIL * (j + 1), GROUP - 1])
                    nc.vector.tensor_copy(tiles[0:HD], o[:, 0:QT]).then_inc(ring_free, 1)

                def add_projection(u):
                    b = u % 2
                    if u < 2:
                        dve.wait_ge(xres_in, i * 16 + 16)
                    else:
                        dve.wait_ge(ring_free, ring.done(f"Y{u - 2}"))
                    dve.wait_ge(ring_full, ring.done(f"Y{u}"))
                    nc.vector.scalar_tensor_tensor(out=xres[:, b], in0=ps_ring[:, ring.bank(f"Y{u}")], scalar=tgate[:, 0:1],
                                                   in1=xres[:, b], op0=ALU.mult, op1=ALU.add).then_inc(ring_free, 1)

                for step in steps:
                    n = int(step[1]) if step[1:] else 0
                    if step in ring.split:
                        evacuate(step)
                    elif step[0] == "S":
                        maxima(n)
                    elif step[0] == "R":
                        reciprocals(n)
                    elif step[0] == "P":
                        for t in range(2):
                            dve.wait_ge(pt_high, i * (2 * UNITS) + (2 * n + t + 1))
                            nc.vector.tensor_tensor(pT[:, LOW, t], ps_pt[:, t], pT[:, HIGH, t].bitcast(F32), ALU.subtract).then_inc(pt_low, 1)
                    elif step[0] == "O":
                        attention_out(n)
                    elif step[0] == "Y":
                        add_projection(n)
                    elif step[0] == "D" and n < blocks:
                        unpack(i, last, n)
                        if n + 2 < blocks:
                            indices(i, last, n + 2)
                    elif step == "L":
                        layer_norm(i + 1, i * 32 + 64)
                    elif step == "A":
                        layer_norm_apply(i + 1)
                    elif step[0] == "N":
                        if n == 0:
                            dve.wait_ge(x1_in, 16)
                        ffn_norm(n, x1n[:, 2 * n:2 * n + 2])
                    elif step[0] == "T":
                        ffn_norm_apply(n, x1n[:, 2 * n:2 * n + 2], x1n[:, 2 * n:2 * n + 2])
                    elif step[0] == "W":
                        split_gu(n)

            def body(i, last):
                indices(i, last, 0)
                indices(i, last, 1)
                follow(i, last, pair_steps(last))

            follow(-1, False, PRO_STEPS)
            with dve.Fori(0, PAIRS - 1, 1) as i:
                body(i, False)
            body(PAIRS - 1, True)

            dve.wait_ge(ring_free, ATT_JOBS)
            ffn_norm(BATCH // 2 - 1, xres)
            ffn_norm_apply(BATCH // 2 - 1, xres, x1n)

            def split_d(n):
                w = P if n < NT - 1 else LAST_N
                dve.wait_ge(d_high, n + 1)
                nc.vector.tensor_tensor(wd[0:w, n, LOW], st_d[0:w, n % 2], wd[0:w, n, HIGH].bitcast(F32),
                                        ALU.subtract).then_inc(d_low, 1)

            for hf in range(2):
                for n in range(NT):
                    w, at = (P if n < NT - 1 else LAST_N), hf * NT + n
                    dve.wait_ge(silu_done, at + 1)
                    dve.wait_ge(u_full, at + 1)
                    nc.vector.tensor_tensor(silu[0:w, at % 2], ps_scores[0:w, at % 2, 512:1024], silu[0:w, at % 2], ALU.mult).then_inc(h_done, 1)
                    if hf == 0:
                        if n == 0:
                            for m in range(EARLY, BATCH):
                                x_low(m, ATT_SPLIT + m - EARLY + 1, (ATT_BANK + m - EARLY) % 2)
                        split_d(n)
                    dve.wait_ge(h_high, at + 1)
                    nc.vector.tensor_tensor(hidden[0:w, at % 2, LOW], silu[0:w, at % 2],
                                            hidden[0:w, at % 2, HIGH].bitcast(F32), ALU.subtract).then_inc(h_low, 1)
                    if hf == 0 and n + W_EARLY < NT:
                        split_gu(n + W_EARLY)
                dve.wait_ge(res_in, 16 * (hf + 1))
                for m in range(4):
                    dve.wait_ge(f_y_full, hf * 4 + m + 1)
                    bank = ps_pt[:, m] if m < 2 else ps_ring[:, m - 2]
                    nc.vector.scalar_tensor_tensor(out=res[:, m], in0=bank, scalar=tgate[:, 1:2], in1=res[:, m],
                                                   op0=ALU.mult, op1=ALU.add).then_inc(f_y_free, 1)

        @block.tensor
        def _(pe):
            pe.wait_ge(const_ready, 2)

            def transpose_job(job, tiles):
                if job >= 2:
                    pe.wait_ge(ring_free, job - 1)
                for c, t in enumerate(tiles):
                    op = nc.tensor.transpose(ps_ring[:, job % 2, c * P:(c + 1) * P], t, ident[:])
                op.then_inc(ring_full, 1)

            pe.wait_ge(wk_in, 32)
            for t in range(QT):
                transpose_job(t, [wk_raw[:, t, c * P:(c + 1) * P] for c in range(DC)])
            pe.wait_ge(wv_in, 16)
            for t in range(QT):
                transpose_job(QT + t, [wv_raw[:, t, c * P:(c + 1) * P] for c in range(DC)])
            pe.wait_ge(wq_in, 32 * KV)
            for t in range(KV * QT):
                transpose_job(2 * QT + t, [wq_raw[:, t, c * P:(c + 1) * P] for c in range(DC)])
            pe.wait_ge(wo_in, 32 * KV * DC)
            for t in range(KV * QT):
                transpose_job(2 * QT + KV * QT + t, [wo_raw[:, b, t] for b in range(DC)])

            def transpose_x(m, bank):
                pe.wait_ge(f_ln, m // 2 + 1)
                for c in range(DC):
                    op = nc.tensor.transpose(bank[:, c * P:(c + 1) * P], x1n[:, m % EARLY, c * P:(c + 1) * P], ident[:])
                return op

            def follow(i, steps):
                ring = Ring(i, steps)

                def open_slot(job):
                    pe.wait_ge(ring_free, ring.slot(job))
                    return ps_ring[:, ring.bank(job)]

                def product(dst, stationary, moving):
                    for c in range(DC):
                        for n, (a, b) in enumerate(PASSES):
                            op = nc.tensor.matmul(dst, stationary(a, c), moving(b, c), start=(c == 0 and n == 0),
                                                  stop=(c == DC - 1 and n == len(PASSES) - 1))
                    return op

                def project(job):
                    bank = open_slot(job)
                    if job[0] == "K":
                        cols = slice(int(job[1]) * P, (int(job[1]) + 1) * P)
                        op = product(bank, lambda a, c: wkT[:, a, c, cols], lambda b, c: hT[:, b, c])
                    elif job[0] == "V":
                        m = int(job[1])
                        op = product(bank[:, 0:KV * HD], lambda a, c: hT[:, a, c, m], lambda b, c: wvT[:, b, c])
                    elif job[0] == "Q":
                        t = int(job[1]) * QT + int(job[3])
                        op = product(bank[:, 0:2 * TOK], lambda a, c: wqT[:, a, c, t * P:(t + 1) * P],
                                     lambda b, c: hT[:, b, c, 0:2])
                    elif job[0] == "X":
                        op = transpose_x(int(job[1]), bank)
                    else:
                        m = int(job[1])
                        if m == 0:
                            pe.wait_ge(ln_done, i + 2)
                            pe.wait_ge(x_in, i * 32 + 64)
                        for c in range(DC):
                            op = nc.tensor.transpose(bank[:, c * P:(c + 1) * P], xin[:, m, c * P:(c + 1) * P], ident[:])
                    op.then_inc(ring_full, 1)

                def scores(u):
                    kv, b = u // 2 % KV, u % 2
                    if u == UNITS:
                        pe.wait_ge(ring_free, ring.done("K2"))
                    elif u == 2:
                        pe.wait_ge(ring_free, ring.first)
                    elif b == 0:
                        pe.wait_ge(ring_free, ring.done(f"Q{kv}.2"))
                    q = slice(b * TOK, (b + 1) * TOK)
                    s = slice(b * 256, (b + 1) * 256)
                    for h in range(GROUP):
                        for n, (pa, pb) in enumerate(PASSES):
                            stat = qT[kv % 2][0:HD, pa, h, q] if h < QT else q3T[kv % 2][0:HD, pa, q]
                            mov = kT[0:HD, pb, kv, s] if kv < QT else k3T[0:HD, pb, s]
                            op = nc.tensor.matmul(ps_scores[:, b, h * 256:(h + 1) * 256], stat, mov, start=(n == 0),
                                                  stop=(n == len(PASSES) - 1), skip_group_check=True)
                    op.then_inc(s_full, 1)

                def transpose_probs(u):
                    pe.wait_ge(normed, i * UNITS + (u + 1))
                    for t in range(2):
                        for h in range(GROUP):
                            op = nc.tensor.transpose(ps_pt[:, t, h * P:(h + 1) * P], probs[:, u % 2, h, t * P:(t + 1) * P], ident[:])
                        op.then_inc(pt_full, 1)

                def attend(u):
                    kv, b = u // 2, u % 2
                    bank = open_slot(f"O{u}")
                    if u == 0:
                        pe.wait_ge(ring_free, ring.done("V3"))
                    for t in range(2):
                        pe.wait_ge(pt_low, i * (2 * UNITS) + (2 * u + t + 1))
                        block_ = b if t == 0 else 2 + b
                        for n, (pa, pb) in enumerate(PASSES):
                            op = nc.tensor.matmul(bank[0:HD], v_sb[:, pa, block_, kv * HD:(kv + 1) * HD], pT[:, pb, t],
                                                  start=(t == 0 and n == 0), stop=(t == 1 and n == len(PASSES) - 1))
                    op.then_inc(ring_full, 1)

                def project_out(u):
                    bank = open_slot(f"Y{u}")
                    pe.wait_ge(ring_free, ring.done(f"O{u}"))
                    for j in range(QT):
                        op = nc.tensor.matmul(bank, oT[:, u % 2, j], woT[:, u // 2 * QT + j], start=(j == 0), stop=(j == QT - 1))
                    op.then_inc(ring_full, 1)

                for step in steps:
                    if step in ring.split:
                        project(step)
                    elif step[0] in "SPOY":
                        {"S": scores, "P": transpose_probs, "O": attend, "Y": project_out}[step[0]](int(step[1]))

            def body(i, last):
                follow(i, pair_steps(last))

            follow(-1, PRO_STEPS)
            with pe.Fori(0, PAIRS - 1, 1) as i:
                body(i, False)
            body(PAIRS - 1, True)

            def down_tile(hf, n):
                w, at = (P if n < NT - 1 else LAST_N), hf * NT + n
                pe.wait_ge(h_low, at + 1)
                if hf == 0:
                    pe.wait_ge(d_low, n + 1)
                if n == 0:
                    if hf == 0:
                        pe.wait_ge(ring_free, ATT_JOBS + BATCH - EARLY)
                    else:
                        pe.wait_ge(f_y_free, 4)
                for m in range(4):
                    bank = ps_pt[:, m] if m < 2 else ps_ring[:, m - 2]
                    for k, (a, b) in enumerate(PASSES):
                        op = nc.tensor.matmul(bank, hidden[0:w, at % 2, a, m * P:(m + 1) * P], wd[0:w, n, b],
                                              start=(n == 0 and k == 0), stop=(n == NT - 1 and k == len(PASSES) - 1))
                    if n == NT - 1:
                        op.then_inc(f_y_full, 1)
                if n < NT - 1:
                    op.then_inc(down_done, 1)

            for hf in range(2):
                tokens = slice(hf * 512, (hf + 1) * 512)
                for n in range(NT):
                    w, at = (P if n < NT - 1 else LAST_N), hf * NT + n
                    if hf == 0:
                        pe.wait_ge(gu_low, n + 1)
                    if at == 0:
                        pe.wait_ge(ring_free, ATT_JOBS)
                    for mat, full, cols in ((0, g_full, 0), (1, u_full, 512)):
                        if at >= 2:
                            pe.wait_ge(silu_done if mat == 0 else h_done, at - 1)
                        for c in range(DC):
                            for k, (a, b) in enumerate(PASSES):
                                op = nc.tensor.matmul(ps_scores[0:w, at % 2, cols:cols + 512],
                                                      wgu[:, n, a, mat, c, 0:w], x2T[:, b, c, tokens],
                                                      start=(c == 0 and k == 0), stop=(c == DC - 1 and k == len(PASSES) - 1))
                        op.then_inc(full, 1)
                    if at == 0:
                        for m in range(EARLY, BATCH):
                            transpose_x(m, ps_ring[:, (ATT_BANK + m - EARLY) % 2]).then_inc(ring_full, 1)
                    if n > 0:
                        down_tile(hf, n - 1)
                down_tile(hf, NT - 1)


_INS = ["x", "ctx_4096", "g_xattn", "g_ffn", "L0_xattn_Wq", "L0_xattn_Wk", "L0_xattn_Wv", "L0_xattn_Wo"] + [
    f"L0_ffn_{m}_{w}" for m in ("gate", "up", "down") for w in ("qweight", "scales", "qzeros", "g_idx")]


def kernel(**inputs):
    import numpy as _np
    import concourse.bacc as _bacc
    from concourse import mybir as _mybir
    from concourse.bass_utils import run_bass_kernel_spmd as _run

    nc = _bacc.Bacc("TRN2", target_bir_lowering=False, num_devices=1)
    arrays, args = {}, []
    for name in _INS:
        a = _np.ascontiguousarray(inputs[name])
        arrays[f"in_{name}_dram"] = a
        args.append(nc.dram_tensor(f"in_{name}_dram", a.shape, _mybir.dt.from_np(a.dtype), kind="ExternalInput").ap())
    out = nc.dram_tensor("out_0_dram", (BATCH, TOK, D), F32, kind="ExternalOutput").ap()
    build(nc, *args[:8], args[8:12], args[12:16], args[16:20], out)
    r = _run(nc, [arrays], core_ids=[0])
    return r.results[0]["out_0_dram"]
```

```python
from contextlib import ExitStack

import concourse.bass as bass
from concourse import mybir

F32 = mybir.dt.float32
F32R = mybir.dt.float32r
I32 = mybir.dt.int32
ALU = mybir.AluOpType
ACT = mybir.ActivationFunctionType
AX = mybir.AxisListType

P = 128
BATCH, TOK, D = 8, 128, 512
HEADS, KV, HD = 16, 4, 96
GROUP = HEADS // KV
DC = D // P
PAIRS = BATCH // 2
QT = 3
TAIL = 32
INTER = 1376
NT = (INTER + P - 1) // P
LAST_N = INTER - (NT - 1) * P
SCALE = float(HD) ** -0.5
EPS = 1e-5
HIGH, LOW = 0, 1
PASSES = ((HIGH, HIGH), (HIGH, LOW), (LOW, HIGH))

PACK = 8
ZB = 2
NB = INTER // ZB
GATE_GROUPS, DOWN_GROUPS = D // P, INTER // P

UNITS = 2 * KV
PRO_STEPS = """
    k1 k0 k2 H0 H1 H2 H3 K0 q0 K1 q1 K2 q2 Q0.0 v0 Q0.1 v1 Q0.2 v2 q3 q4 q5 Z
    q7 Q1.0 q8 q6 q9 q10 q11 o6 o7 o10 o8 o9 o11 Q1.1 S8 Q1.2 S9 o0 o1 o2 o3 o4 o5 E8 R8 E9""".split()
PAIR_STEPS = """
    V0 V1 R1 V2 V3
    P0 Q2.0 S2 D0 O0 E2 R2 Q2.1
    P1 Q2.2 S3 D1 O1 E3 Y0 R3 L
    P2 Q3.0 Q3.1 S4 D2 O2 E4 Y1 R4 A
    P3 Q3.2 H0 S5 D3 O3 E5 Y2 R5
    P4 H1 H2 S6 H3 D4 O4 E6 Y3 R6
    P5 Q0.0 Q0.1 S7 D5 O5 E7 Y4 R7 Q0.2
    P6 K0 K1 D6 K2 O6 P7 Y5 O7 S8 Y6 Q1.0 E8 Q1.1 Y7 R8 Q1.2 S9 E9""".split()
LAST_STEPS = """
    V0 V1 N0 R1 V2 N1 V3
    P0 Q2.0 S2 D0 O0 E2 R2 Q2.1
    P1 Q2.2 S3 D1 O1 E3 Y0 R3 T0
    P2 Q3.0 Q3.1 S4 D2 O2 E4 Y1 R4 N2
    P3 Q3.2 S5 D3 O3 E5 Y2 R5
    P4 S6 D4 O4 Y3 E6 R6 T1
    P5 S7 D5 O5 E7 R7 Y4 X0 X1 T2
    P6 Y5 O6 W0 X2 X3 P7 Y6 O7 G U W1 X4 X5 Y7""".split()
EARLY = 6
WARM_UP = 24
W_EARLY = 2


def pair_steps(last):
    return LAST_STEPS if last else PAIR_STEPS


def ring_jobs(steps):
    return [s for s in steps if s[0] in "VQHKOYkvqo"]


PRO_JOBS = len(ring_jobs(PRO_STEPS))
PRO_SPLIT = PRO_JOBS
PAIR_JOBS = len(ring_jobs(pair_steps(False)))
PAIR_SPLIT = PAIR_JOBS - UNITS
ATT_JOBS = PRO_JOBS + (PAIRS - 1) * PAIR_JOBS + len(ring_jobs(pair_steps(True)))


class Ring:

    def __init__(self, i, steps):
        self.jobs = ring_jobs(steps)
        self.split = [j for j in self.jobs if j[0] != "Y"]
        self.prologue = isinstance(i, int) and i < 0
        if self.prologue:
            self.first, self.first_split, self.depth = 0, 0, 4
        else:
            self.first, self.first_split, self.depth = i * PAIR_JOBS + PRO_JOBS, i * PAIR_SPLIT + PRO_SPLIT, 2

    def bank(self, job):
        return self.jobs.index(job) % self.depth

    def done(self, job):
        return self.first + (self.jobs.index(job) + 1)

    def slot(self, job):
        n = self.jobs.index(job)
        if self.prologue:
            return max(n - 3, 0)
        return self.first + (n - 1) if n else self.first

    def high(self, job):
        return self.first_split + (self.split.index(job) + 1)


def dequant_blocks(i, last):
    out = [("gate", 0, i, P), ("gate", 1, i, P), ("up", 0, i, P), ("up", 1, i, P)]
    for k in range(3):
        if last and 3 * i + k >= NT:
            continue
        rows = LAST_N if last and 3 * i + k == NT - 1 else P
        out.append(("down", 0, i * 3 + k, rows))
    return out


BLOCKS_PER_PAIR = 7
ZROWS = GATE_GROUPS * ZB
ZTAB = 2 * ZROWS + DOWN_GROUPS


def build(nc, x, ctx, g_xattn, g_ffn, Wq, Wk, Wv, Wo, gate, up, down, out):
    quant = {"gate": gate, "up": up, "down": down}
    with ExitStack() as top:
        def sem(name):
            return top.enter_context(nc.semaphore(name))

        def sbuf(stack, name, shape, dt=F32):
            return stack.enter_context(nc.sbuf_tensor(name, shape, dt))

        x1_scratch = nc.dram_tensor("x1_scratch", (BATCH, TOK, D), F32, kind="Internal").ap()
        wgu_scratch = nc.dram_tensor("wgu_scratch", (2, DC, P, INTER), F32, kind="Internal").ap()
        wo_scratch = nc.dram_tensor("wo_scratch", (KV, P, 2, QT, D), F32, kind="Internal").ap()
        wd_scratch = nc.dram_tensor("wd_scratch", (NT * P, D), F32, kind="Internal").ap()
        table_gu = nc.dram_tensor("table_gu", (2, GATE_GROUPS * ZB, 2, NB), F32, kind="Internal").ap()
        table_d = nc.dram_tensor("table_d", (DOWN_GROUPS, 2, D), F32, kind="Internal").ap()

        ps_scores = top.enter_context(nc.psum_tensor("ps_scores", [P, 2, GROUP * 256], F32))
        ps_pt = top.enter_context(nc.psum_tensor("ps_pt", [P, 2, 512], F32))
        ps_ring = top.enter_context(nc.psum_tensor("ps_ring", [P, 2, 512], F32))

        ident = sbuf(top, "ident", [P, P])
        gates = sbuf(top, "gates", [P, 2])
        tgate = sbuf(top, "tgate", [P, 2])
        neg_half = sbuf(top, "neg_half", [P, BATCH])
        bn = sbuf(top, "bn", [P, BATCH, 6])
        mv = sbuf(top, "mv", [P, BATCH, 2])
        veps = sbuf(top, "veps", [P, BATCH])
        rstd = sbuf(top, "rstd", [P, BATCH])
        xres = sbuf(top, "xres", [P, 2, D])

        att = ExitStack()
        wqT = sbuf(att, "wqT", [P, 2, DC, HEADS * HD], F32R)
        wkT = sbuf(att, "wkT", [P, 2, DC, KV * HD], F32R)
        wvT = sbuf(att, "wvT", [P, 2, DC, KV * HD], F32R)
        hT = sbuf(att, "hT", [P, 2, DC, 4, P], F32R)
        xin = sbuf(att, "xin", [P, 4, D])
        kT = sbuf(att, "kT", [P, 2, QT, 512], F32R)
        k3T = sbuf(att, "k3T", [P, 2, 512], F32R)
        qT = [sbuf(att, f"qT{n}", [P, 2, QT, 2 * TOK], F32R) for n in range(2)]
        q3T = [sbuf(att, f"q3T{n}", [P, 2, 2 * TOK], F32R) for n in range(2)]
        probs = sbuf(att, "probs", [P, 2, GROUP, 256])
        pT = sbuf(att, "pT", [P, 2, 2, 512], F32R)
        v_sb = sbuf(att, "v_sb", [P, 2, 4, KV * HD], F32R)
        woT = [sbuf(att, f"woT{n}", [P, 2, QT, D], F32R) for n in range(2)]
        oT = sbuf(att, "oT", [P, 2, 2, QT, TOK], F32R)
        dq_t = sbuf(att, "dq_t", [P, 2, 2 * NB])
        dq_q = sbuf(att, "dq_q", [P, 2, NB], I32)
        gidx_i = sbuf(att, "gidx_i", [P, 2 * DC + NT], I32)
        gidx = sbuf(att, "gidx", [P, 2 * DC + NT])
        gneg = sbuf(att, "gneg", [P, 2 * DC + NT])
        idx = sbuf(att, "idx", [P, 2], I32)
        shift_row = sbuf(att, "shift_row", [P, 1], I32)
        shift_col = sbuf(att, "shift_col", [P, PACK], I32)
        rowno = sbuf(att, "rowno", [P, 1], I32)
        negmax = sbuf(att, "negmax", [P, 2, GROUP])
        sums = sbuf(att, "sums", [P, 2, GROUP])
        rsums = sbuf(att, "rsums", [P, 2, GROUP])
        att.close()
        with ExitStack() as before:
            room = (2 * DC * (HEADS + 2 * KV) * HD + 2 * DC * 4 * P
                    + 4 * D + 2 * (QT + 1) * 512
                    + 2 * (QT + 1) * 4 * TOK + GROUP * 256)
            sbuf(before, "room_before", [P, room])
            wo_raw = sbuf(before, "wo_raw", [P, DC, HEADS * HD])
            wq_raw = sbuf(before, "wq_raw", [P, KV * QT, D])
            wk_raw = sbuf(before, "wk_raw", [P, QT, D])
            wv_raw = sbuf(before, "wv_raw", [P, QT, D])

        with ExitStack() as early:
            sbuf(early, "room_of_wqT", [P, 2, DC, HEADS * HD])
            x1n = sbuf(early, "x1n", [P, EARLY, D])
        ffn = ExitStack()
        wgu = sbuf(ffn, "wgu", [P, NT, 2, 2, DC, P], F32R)
        st_gu = sbuf(ffn, "st_gu", [P, 2, 2, DC, P])
        x2T = sbuf(ffn, "x2T", [P, 2, DC, BATCH * TOK], F32R)
        wd = sbuf(ffn, "wd", [P, NT, 2, D], F32R)
        hidden = sbuf(ffn, "hidden", [P, 2, 2, 512], F32R)
        silu = sbuf(ffn, "silu", [P, 2, 512])
        res = sbuf(ffn, "res", [P, 4, D])
        st_d = sbuf(ffn, "st_d", [P, 2, D])
        ffn.close()

        const_ready = sem("const_ready")
        shifts_ready = sem("shifts_ready")
        wk_in, wv_in, wo_in = sem("wk_in"), sem("wv_in"), sem("wo_in")
        wq_in = [sem(f"wq_in{kv}") for kv in range(KV)]
        small_in = sem("small_in")
        wo_stored = [sem("wo_stored0"), sem("wo_stored1")]
        wo_there = [sem("wo_there0"), sem("wo_there1")]
        x_in, ctx_in = sem("x_in"), sem("ctx_in")
        ln_stat = sem("ln_stat")
        ln_var = sem("ln_var")
        ln_rstd = sem("ln_rstd")
        ln_done = sem("ln_done")
        tanh_done = sem("tanh_done")
        ring_full, ring_high, ring_free = sem("ring_full"), sem("ring_high"), sem("ring_free")
        s_full, maxed, expd, recip, normed = (sem(n) for n in ("s_full", "maxed", "expd", "recip", "normed"))
        pt_full, pt_high, pt_low = sem("pt_full"), sem("pt_high"), sem("pt_low")
        xres_in, x1_out = sem("xres_in"), sem("x1_out")
        gi_chain = sem("gi_chain")
        zraw_clear, zraw_in, table_out, z_chain = (sem(n) for n in ("zraw_clear", "zraw_in", "table_out", "z_chain"))
        gathered, q_in = [sem("gathered0"), sem("gathered1")], [sem("q_in0"), sem("q_in1")]
        idx_ready, unpacked, w_ready, w_out, dq_chain = (
            sem(n) for n in ("idx_ready", "unpacked", "w_ready", "w_out", "dq_chain"))
        stage_in = [sem("stage_in0"), sem("stage_in1")]
        stage_d_in = [sem("stage_d_in0"), sem("stage_d_in1")]
        gu_high, gu_low, d_high, d_low = (sem(n) for n in ("gu_high", "gu_low", "d_high", "d_low"))
        xt_full, xt_high, xt_low = sem("xt_full"), sem("xt_high"), sem("xt_low")
        passed_v, passed_p = sem("passed_v"), sem("passed_p")
        x1_in = [sem(f"x1_in{k}") for k in range(EARLY // 2)]
        f_stat, f_mv, f_var, f_rstd, f_ln = (sem(n) for n in ("f_stat", "f_mv", "f_var", "f_rstd", "f_ln"))
        g_full, u_full, silu_done, h_done, h_high, h_low, down_done = (
            sem(n) for n in ("g_full", "u_full", "silu_done", "h_done", "h_high", "h_low", "down_done"))
        f_y_full, f_y_free = sem("f_y_full"), sem("f_y_free")
        res_in, o_out = sem("res_in"), sem("o_out")

        block = top.enter_context(nc.Block())

        def x_bank(m):
            return ps_scores[:, int(m in (4, 5)), m % 2 * 512:m % 2 * 512 + 512]

        def ring_bank(n):
            return ps_ring[:, n] if n < 2 else ps_pt[:, n - 2]

        def in_rows(src, i):
            return src[bass.ds(i * 2, 2)].rearrange("b p d -> p b d")

        @block.sync
        def _(sp):
            sp.dma_start(xin[:, 0:2, :], in_rows(x, 0)).then_inc(x_in, 16)
            sp.dma_start(wk_raw[0:HD], Wk[0:QT * HD].rearrange("(j p) d -> p j d", p=HD)).then_inc(wk_in, 16)
            sp.dma_start(wk_raw[HD:P], Wk[QT * HD:].rearrange("(j p) d -> p j d", p=TAIL)).then_inc(wk_in, 16)
            sp.dma_start(xin[:, 2:4, :], in_rows(ctx, 0)).then_inc(ctx_in, 16)
            for kv in range(KV):
                rows, dst = Wq[kv * GROUP * HD:(kv + 1) * GROUP * HD], wq_raw[:, kv * QT:(kv + 1) * QT]
                sp.dma_start(dst[0:HD], rows[0:QT * HD].rearrange("(j p) d -> p j d", p=HD)).then_inc(wq_in[kv], 16)
                sp.dma_start(dst[HD:P], rows[QT * HD:].rearrange("(j p) d -> p j d", p=TAIL)).then_inc(wq_in[kv], 16)
                if kv == 0:
                    sp.dma_start(wv_raw[:], Wv.rearrange("(j p) d -> p j d", p=P)).then_inc(wv_in, 16)
            sp.dma_start(wo_raw[:], Wo.rearrange("(b p) e -> p b e", p=P)).then_inc(wo_in, 16)
            sp.dma_start(xres[:], in_rows(x, 0)).then_inc(xres_in, 16)

            pro = Ring(-1, PRO_STEPS)

            def store_wo(kv, done):
                sp.wait_ge(ring_free, pro.done(f"o{kv * QT + QT - 1}"))
                sp.dma_start(wo_scratch[kv], woT[kv % 2][:].bitcast(F32)).then_inc(done, 16)

            sp.wait_ge(zraw_clear, 1)
            for m, name in enumerate(("gate", "up")):
                sp.dma_start(dq_q[m * ZROWS:(m + 1) * ZROWS, 0, 0:NB // PACK],
                             quant[name][2].rearrange("g (b n) -> (g b) n", b=ZB)).then_inc(zraw_in, 16)
                sp.dma_start(table_gu[m, :, 0, :], quant[name][1].rearrange("g (b n) -> (g b) n", b=ZB)).then_inc(table_out, 16)
            sp.dma_start(dq_q[2 * ZROWS:2 * ZROWS + DOWN_GROUPS, 0, 0:D // PACK], down[2]).then_inc(zraw_in, 16)
            sp.dma_start(table_d[:, 0, :], down[1]).then_inc(table_out, 16)
            sp.wait_ge(z_chain, 2)
            zeros = dq_t[:, 1]
            for m in range(2):
                sp.dma_start(table_gu[m, :, 1, :], zeros[m * ZROWS:(m + 1) * ZROWS, 0:NB]).then_inc(table_out, 16)
            sp.dma_start(table_d[:, 1, :], zeros[2 * ZROWS:2 * ZROWS + DOWN_GROUPS, 0:D]).then_inc(table_out, 16)

            store_wo(2, wo_stored[0])
            store_wo(3, wo_stored[1])
            store_wo(0, wo_there[0])
            store_wo(1, wo_there[1])

            def raw_block(i, last, k):
                name, cb, t, rows = dequant_blocks(i, last)[k]
                qw = quant[name][0]
                width, cols = (NB, INTER) if name != "down" else (D, D)
                if k >= 2:
                    sp.wait_ge(w_out, i * (BLOCKS_PER_PAIR * 16) + (k - 1) * 16)
                src = bass.AP(qw.tensor, t * (P // PACK * cols) + cb * NB, [[cols, rows // PACK], [0, PACK], [1, width]])
                sp.dma_start(dq_q[0:rows, k % 2, 0:width], src).then_inc(q_in[k % 2], 16)

            def store_block(i, last, k):
                name, cb, t, rows = dequant_blocks(i, last)[k]
                sp.wait_ge(w_ready, i * BLOCKS_PER_PAIR + (k + 1))
                if name == "down":
                    dst = wd_scratch[bass.ds(t * P, rows)]
                    sp.dma_start(dst, dq_q[0:rows, k % 2, 0:D].bitcast(F32)).then_inc(w_out, 16)
                else:
                    dst = wgu_scratch[("gate", "up").index(name)].rearrange("c p n -> (c p) n")
                    sp.dma_start(dst[bass.ds(t * P, P), cb * NB:(cb + 1) * NB], dq_q[:, k % 2].bitcast(F32)).then_inc(w_out, 16)

            def load_gu(n):
                w = P if n < NT - 1 else LAST_N
                if n >= 2:
                    sp.wait_ge(gu_low, n - 1)
                for m in range(2):
                    src = wgu_scratch[m, :, :, n * P:n * P + w].rearrange("c p n -> p c n")
                    sp.dma_start(st_gu[:, n % 2, m, :, 0:w], src).then_inc(stage_in[n % 2], 16)

            def load_d(n):
                w = P if n < NT - 1 else LAST_N
                if n >= 2:
                    sp.wait_ge(d_low, n - 1)
                sp.dma_start(st_d[0:w, n % 2], wd_scratch[n * P:n * P + w]).then_inc(stage_d_in[n % 2], 16)

            def body(i, last):
                ring = Ring(i, pair_steps(last))
                blocks = len(dequant_blocks(i, last))
                if last:
                    sp.wait_ge(ring_full, ring.first)
                    for k in range(EARLY // 2):
                        sp.dma_start(x1n[:, 2 * k:2 * k + 2], x1_scratch[2 * k:2 * k + 2].rearrange("m p d -> p m d")).then_inc(x1_in[k], 16)
                if not last:
                    sp.wait_ge(ring_full, ring.first)
                    sp.dma_start(xin[:, 0:2, :], in_rows(x, i + 1)).then_inc(x_in, 16)
                    sp.dma_start(xin[:, 2:4, :], in_rows(ctx, i + 1)).then_inc(ctx_in, 16)
                raw_block(i, last, 0)
                raw_block(i, last, 1)
                for k in range(blocks):
                    store_block(i, last, k)
                    if k + 2 < blocks:
                        raw_block(i, last, k + 2)
                    if last and k == 3:
                        load_gu(0)
                        load_gu(1)
                if last:
                    load_gu(2)
                for b in range(2):
                    sp.wait_ge(ring_free, ring.done(f"Y{UNITS - 2 + b}"))
                    sp.dma_start(x1_scratch[bass.ds(i * 2 + b, 1)].rearrange("b p d -> (b p) d"), xres[:, b]).then_inc(x1_out, 16)
                if not last:
                    sp.wait_ge(w_out, i * (BLOCKS_PER_PAIR * 16) + BLOCKS_PER_PAIR * 16)
                    sp.wait_ge(x1_out, i * 32 + 32)
                    sp.dma_start(xres[:], in_rows(x, i + 1)).then_inc(xres_in, 16)

            with sp.Fori(0, PAIRS - 1, 1) as i:
                body(i, False)
            body(PAIRS - 1, True)

            sp.wait_ge(w_out, 16 * (BLOCKS_PER_PAIR * PAIRS - 1))
            sp.wait_ge(ring_free, ATT_JOBS)
            load_d(0)
            load_d(1)

            def load_res(hf):
                sp.dma_start(res[:], x1_scratch[hf * 4:hf * 4 + 4].rearrange("m p d -> p m d")).then_inc(res_in, 16)

            sp.wait_ge(x1_out, PAIRS * 32)
            load_res(0)
            for n in range(3, NT):
                load_gu(n)
                load_d(n - 1)
            load_d(NT - 1)
            for hf in range(2):
                if hf == 1:
                    sp.wait_ge(o_out, 64)
                    load_res(1)
                for m in range(4):
                    sp.wait_ge(f_y_free, hf * 4 + m + 1)
                    sp.dma_start(out[hf * 4 + m], res[:, m]).then_inc(o_out, 16)
            sp.wait_ge(o_out, 16 * BATCH)

        @block.gpsimd
        def _(pool):
            nc.gpsimd.memset(ident[:], 0.0).then_inc(const_ready, 1)
            pool.wait_ge(const_ready, 1)
            nc.gpsimd.affine_select(out=ident[:], in_=ident[:], compare_op=ALU.not_equal, fill=1.0, base=0,
                                    pattern=[[-1, P]], channel_multiplier=1).then_inc(const_ready, 1)
            nc.gpsimd.memset(neg_half[:], -0.5).then_inc(const_ready, 1)
            nc.gpsimd.iota(rowno[:], pattern=[[0, 1]], base=0, channel_multiplier=1).then_inc(const_ready, 1)
            nc.gpsimd.iota(shift_col[:], pattern=[[4, PACK]], base=0, channel_multiplier=0).then_inc(const_ready, 1)

            def ln_power(n):
                pool.wait_ge(ln_var, n)
                nc.gpsimd.tensor_tensor(out=rstd[:, 0:2], in0=veps[:, 0:2], in1=neg_half[:, 0:2], op=ALU.pow).then_inc(ln_rstd, 1)

            def ffn_power(k):
                pool.wait_ge(f_var, k + 1)
                cols = slice(2 * k, 2 * k + 2)
                nc.gpsimd.tensor_tensor(out=rstd[:, cols], in0=veps[:, cols], in1=neg_half[:, cols], op=ALU.pow).then_inc(f_rstd, 1)

            def carry():
                pool.sem_inc(passed_p, 1)

            def normalise(i, u):
                pool.wait_ge(recip, i * UNITS + (u + 1))
                carry()
                for h in range(GROUP):
                    op = nc.gpsimd.tensor_scalar(probs[:, u % 2, h], probs[:, u % 2, h], rsums[:, u % 2, h:h + 1], 1.0,
                                                 ALU.mult, ALU.mult)
                op.then_inc(normed, 1)

            def gather(i, last, k):
                name, cb, t, rows = dequant_blocks(i, last)[k]
                width = NB if name != "down" else D
                table = table_d if name == "down" else table_gu.rearrange("m g t n -> (m g) t n")
                pool.wait_ge(idx_ready, i * BLOCKS_PER_PAIR + (k + 1))
                if k >= 2:
                    pool.wait_ge(w_ready, i * BLOCKS_PER_PAIR + (k - 1))
                carry()
                at = bass.IndirectOffsetOnAxis(ap=idx[0:rows, k % 2:k % 2 + 1], axis=0)
                nc.gpsimd.indirect_dma_start(dq_t[0:rows, k % 2, 0:2 * width], None, table.rearrange("g t n -> g (t n)"), at).then_inc(gathered[k % 2], 16)

            def rescale(i, last, k):
                name, cb, t, rows = dequant_blocks(i, last)[k]
                width = NB if name != "down" else D
                pool.wait_ge(unpacked, i * BLOCKS_PER_PAIR + (k + 1))
                w = dq_q[0:rows, k % 2, 0:width].bitcast(F32)
                nc.gpsimd.tensor_tensor(out=w, in0=w, in1=dq_t[0:rows, k % 2, 0:width], op=ALU.mult).then_inc(w_ready, 1)

            pool.wait_ge(const_ready, 3)
            ln_power(1)

            pool.wait_ge(table_out, 16 * 6)

            def follow(i, last, steps):
                blocks = len(dequant_blocks(i, last))
                for step in steps:
                    n = int(step[1]) if step[1:] else 0
                    if step[0] == "R":
                        normalise(i, n)
                    elif step[0] == "D" and n < blocks:
                        if n + 1 < blocks:
                            gather(i, last, n + 1)
                        rescale(i, last, n)
                    elif step == "L":
                        ln_power(i + 2)
                    elif step[0] == "N":
                        ffn_power(n)

            def body(i, last):
                gather(i, last, 0)
                follow(i, last, pair_steps(last))
                if not last:
                    pool.wait_ge(w_ready, i * BLOCKS_PER_PAIR + BLOCKS_PER_PAIR)

            follow(-1, False, PRO_STEPS)
            with pool.Fori(0, PAIRS - 1, 1) as i:
                body(i, False)
            body(PAIRS - 1, True)
            ffn_power(BATCH // 2 - 1)

        @block.scalar
        def _(act):
            act.dma_start(gates[:, 0:1], bass.AP(g_xattn.tensor, 0, [[0, P], [1, 1]])).then_inc(small_in, 16)
            act.dma_start(gates[:, 1:2], bass.AP(g_ffn.tensor, 0, [[0, P], [1, 1]])).then_inc(small_in, 16)
            act.wait_ge(gi_chain, 1)
            act.dma_start(gidx_i[:, 0:DC], gate[3].rearrange("(c p) -> p c", p=P), allow_slow_non_contiguous=True).then_inc(small_in, 16)
            act.dma_start(gidx_i[:, DC:2 * DC], up[3].rearrange("(c p) -> p c", p=P), allow_slow_non_contiguous=True).then_inc(small_in, 16)
            act.dma_start(gidx_i[:, 2 * DC:2 * DC + NT - 1],
                           down[3][0:(NT - 1) * P].rearrange("(c p) -> p c", p=P), allow_slow_non_contiguous=True).then_inc(small_in, 16)
            act.dma_start(gidx_i[0:LAST_N, 2 * DC + NT - 1:], down[3][(NT - 1) * P:].rearrange("(c p) -> p c", c=1), allow_slow_non_contiguous=True).then_inc(small_in, 16)

            def high(job_done, bank, dst, cols=512, shape=None, scale=1.0):
                act.wait_ge(ring_full, job_done)
                src = ring_bank(bank)[:, 0:cols]
                if shape:
                    src = src.rearrange(*shape[0], **shape[1])
                if isinstance(dst, list):
                    nc.scalar.activation(dst[1], src[HD:P], ACT.Copy, scale=scale)
                    dst, src = dst[0], src[0:HD]
                nc.scalar.activation(dst, src, ACT.Copy, scale=scale).then_inc(ring_high, 1)

            by_chunk = (("p (c n) -> p c n",), {"c": DC})
            def x_high(m):
                act.wait_ge(xt_full, m + 1)
                nc.scalar.activation(x2T[:, HIGH, :, m * P:(m + 1) * P], x_bank(m).rearrange("p (c n) -> p c n", c=DC),
                                     ACT.Copy).then_inc(xt_high, 1)

            def load_wo(kv):
                act.dma_start(woT[kv % 2][:].bitcast(F32), wo_scratch[kv]).then_inc(wo_there[kv % 2], 16)

            def split_gu(n):
                w = P if n < NT - 1 else LAST_N
                act.wait_ge(stage_in[n % 2], 32 * (n // 2 + 1))
                nc.scalar.activation(wgu[:, n, HIGH, :, :, 0:w], st_gu[:, n % 2, :, :, 0:w], ACT.Copy).then_inc(gu_high, 1)

            def follow(i, steps):
                ring = Ring(i, steps)

                def evacuate(job):
                    done, bank = ring.done(job), ring.bank(job)
                    if job[0] == "K":
                        j = int(job[1])
                        high(done, bank, [kT[0:HD, HIGH, j].rearrange("p (b t s) -> p t b s", b=2, t=2),
                                          k3T[TAIL * j:TAIL * (j + 1), HIGH].rearrange("p (b t s) -> p t b s", b=2, t=2)],
                             shape=(("p (t b s) -> p t b s",), {"b": 2, "t": 2}))
                    elif job[0] == "V":
                        high(done, bank, v_sb[:, HIGH, int(job[1])], KV * HD)
                    elif job[0] == "Q":
                        g, j = int(job[1]) % 2, int(job[3])
                        high(done, bank, [qT[g][0:HD, HIGH, j], q3T[g][TAIL * j:TAIL * (j + 1), HIGH]], 2 * TOK, scale=SCALE)
                    elif job[0] == "o":
                        kv, j = int(job[1:]) // QT, int(job[1:]) % QT
                        if kv < 2 and j == 0:
                            act.wait_ge(wo_stored[kv], 16)
                        high(done, bank, woT[kv % 2][:, HIGH, j])
                    elif job[0] == "O":
                        act.wait_ge(ring_full, done)
                        o, b = ring_bank(bank)[0:HD].rearrange("p (h q) -> p h q", h=GROUP), int(job[1]) % 2
                        for j in range(QT):
                            nc.scalar.activation(oT[HD:P, b, HIGH, j], o[TAIL * j:TAIL * (j + 1), GROUP - 1], ACT.Copy)
                        nc.scalar.activation(oT[0:HD, b, HIGH], o[:, 0:QT], ACT.Copy).then_inc(ring_high, 1)
                    elif job[0] in "kvq":
                        dst, t = {"k": wkT, "v": wvT, "q": wqT}[job[0]], int(job[1:])
                        high(done, bank, dst[:, HIGH, :, t * P:(t + 1) * P], shape=by_chunk)
                    else:
                        high(done, bank, hT[:, HIGH, :, int(job[1]), :], shape=by_chunk)

                def exponentials(u):
                    act.wait_ge(maxed, i * UNITS + (u + 1))
                    for h in range(GROUP):
                        op = nc.scalar.activation(probs[:, u % 2, h], ps_scores[:, u % 2, h * 256:(h + 1) * 256], ACT.Exp,
                                                  bias=negmax[:, u % 2, h:h + 1], accum_out=sums[:, u % 2, h:h + 1])
                    op.then_inc(expd, 1)

                for step in steps:
                    if step in ring.split:
                        evacuate(step)
                    elif step[0] == "E":
                        exponentials(int(step[1]))
                        if step == "E8" and steps is PAIR_STEPS:
                            act.wait_ge(ring_full, ring.done("Y5"))
                            load_wo(0)
                    elif step[0] == "W":
                        split_gu(int(step[1]))
                    elif step[0] == "X":
                        x_high(int(step[1]))
                    elif step == "Z":
                        act.wait_ge(small_in, 96)
                        nc.scalar.activation(tgate[:], gates[:], ACT.Tanh).then_inc(tanh_done, 1)
                    elif step[0] == "P":
                        n = int(step[1])
                        if n == 0:
                            act.wait_ge(ring_full, ring.first)
                            act.wait_ge(wo_there[1], i * 32 + 16)
                            load_wo(1)
                        elif n in (3, 5):
                            act.wait_ge(ring_full, ring.done(f"Y{n - 2}"))
                            load_wo((n + 1) // 2 % KV)
                        for t in range(2):
                            act.wait_ge(pt_full, i * (2 * UNITS) + (2 * int(step[1]) + t + 1))
                            nc.scalar.activation(pT[:, HIGH, t], ps_pt[:, t], ACT.Copy).then_inc(pt_high, 1)

            def body(i, last):
                follow(i, pair_steps(last))

            follow(-1, PRO_STEPS)
            with act.Fori(0, PAIRS - 1, 1) as i:
                body(i, False)
            body(PAIRS - 1, True)

            act.wait_ge(ring_free, ATT_JOBS)
            act.wait_ge(w_ready, BLOCKS_PER_PAIR * PAIRS - 1)

            def split_d(n):
                w = P if n < NT - 1 else LAST_N
                act.wait_ge(stage_d_in[n % 2], 16 * (n // 2 + 1))
                nc.scalar.activation(wd[0:w, n, HIGH], st_d[0:w, n % 2], ACT.Copy).then_inc(d_high, 1)

            for hf in range(2):
                for n in range(NT):
                    w, at = (P if n < NT - 1 else LAST_N), hf * NT + n
                    act.wait_ge(g_full, at + 1)
                    if at >= 2:
                        act.wait_ge(h_low, at - 1)
                    nc.scalar.activation(silu[0:w, at % 2], ps_scores[0:w, at % 2, 0:512], ACT.Silu).then_inc(silu_done, 1)
                    if hf == 0:
                        if n == 1:
                            for m in range(EARLY, BATCH):
                                x_high(m)
                        split_d(n)
                    act.wait_ge(h_done, at + 1)
                    if at == NT + 1:
                        act.wait_ge(f_y_full, 4)
                    elif at >= 2:
                        act.wait_ge(down_done, at - 1 - (at > NT))
                    nc.scalar.activation(hidden[0:w, at % 2, HIGH], silu[0:w, at % 2], ACT.Copy).then_inc(h_high, 1)
                    if hf == 0 and n + W_EARLY < NT:
                        split_gu(n + W_EARLY)

        @block.vector
        def _(dve):
            nc.vector.memset(gidx_i[:], 0).then_inc(gi_chain, 1)
            nc.vector.memset(dq_q[:, 0, 0:NB // PACK], 0).then_inc(zraw_clear, 1)

            def layer_norm(i_next, wait_in):
                dve.wait_ge(x_in, wait_in)
                for m in range(2):
                    nc.vector.bn_stats(bn[:, m], xin[:, m]).then_inc(ln_stat, 1)
                base = i_next * 4
                dve.wait_ge(ln_stat, base + 2)
                dve.sem_inc(passed_v, 1)
                for m in range(2):
                    nc.vector.bn_aggr(mv[:, m], bn[:, m]).then_inc(ln_stat, 1)
                dve.wait_ge(ln_stat, base + 4)
                nc.vector.tensor_scalar(veps[:, 0:2], mv[:, 0:2, 1], EPS, None, ALU.add).then_inc(ln_var, 1)

            def layer_norm_apply(i_next):
                dve.wait_ge(ln_rstd, i_next + 1)
                for m in range(2):
                    op = nc.vector.tensor_scalar(xin[:, m], xin[:, m], mv[:, m, 0:1], rstd[:, m:m + 1], ALU.subtract, ALU.mult)
                op.then_inc(ln_done, 1)

            def low(high_done, bank, dst, hi, cols=512, shape=None, scale=None):
                dve.wait_ge(ring_high, high_done)
                src = ring_bank(bank)[:, 0:cols]
                if shape:
                    src = src.rearrange(*shape[0], **shape[1])

                def rest(dst, src, hi):
                    if scale is None:
                        return nc.vector.tensor_tensor(dst, src, hi.bitcast(F32), ALU.subtract)
                    return nc.vector.scalar_tensor_tensor(out=dst, in0=src, scalar=scale, in1=hi.bitcast(F32), op0=ALU.mult,
                                                          op1=ALU.subtract)

                if isinstance(dst, list):
                    rest(dst[1], src[HD:P], hi[1])
                    dst, hi, src = dst[0], hi[0], src[0:HD]
                rest(dst, src, hi).then_inc(ring_free, 1)

            dve.wait_ge(const_ready, 5)
            nc.vector.tensor_scalar(shift_row[:], rowno[:], PACK - 1, 2, ALU.bitwise_and, ALU.logical_shift_left).then_inc(shifts_ready, 1)
            by_chunk = (("p (c n) -> p c n",), {"c": DC})
            layer_norm(0, 16)
            layer_norm_apply(0)
            def small_work():
                dve.wait_ge(small_in, 96)
                nc.vector.tensor_copy(gidx[:], gidx_i[:]).then_inc(gi_chain, 1)
                dve.wait_ge(gi_chain, 2)
                for cols, groups in ((slice(0, 2 * DC), GATE_GROUPS), (slice(2 * DC, 2 * DC + NT), DOWN_GROUPS)):
                    nc.vector.tensor_scalar(gneg[:, cols], gidx[:, cols], 0.0, float(groups), ALU.is_lt, ALU.mult).then_inc(gi_chain, 1)
                dve.wait_ge(gi_chain, 4)
                nc.vector.tensor_tensor(gidx[:], gidx[:], gneg[:], ALU.add).then_inc(gi_chain, 1)
                dve.wait_ge(gi_chain, 5)
                for cols, groups in ((slice(0, 2 * DC), GATE_GROUPS), (slice(2 * DC, 2 * DC + NT), DOWN_GROUPS)):
                    nc.vector.tensor_scalar(gidx[:, cols], gidx[:, cols], 0.0, float(groups - 1), ALU.max, ALU.min).then_inc(gi_chain, 1)
                dve.wait_ge(gi_chain, 7)
                dve.wait_ge(shifts_ready, 1)
                dve.wait_ge(tanh_done, 1)

                dve.wait_ge(zraw_in, 48)
                zeros = dq_t[0:ZTAB, 1, 0:NB].bitcast(I32)
                nc.vector.tensor_tensor(zeros.rearrange("p (c j) -> p c j", j=PACK),
                                        dq_q[0:ZTAB, 0, 0:NB // PACK].unsqueeze(2).to_broadcast([ZTAB, NB // PACK, PACK]),
                                        shift_col[0:ZTAB].unsqueeze(1).to_broadcast([ZTAB, NB // PACK, PACK]),
                                        ALU.logical_shift_right).then_inc(z_chain, 1)
                dve.wait_ge(z_chain, 1)
                nc.vector.tensor_scalar(zeros, zeros, PACK * 2 - 1, None, ALU.bitwise_and).then_inc(z_chain, 1)

            def indices(i, last, k):
                name, cb, t, rows = dequant_blocks(i, last)[k]
                col = {"gate": 0, "up": DC, "down": 2 * DC}[name] + t
                split = ZB if name != "down" else 1
                cb += ZROWS if name == "up" else 0
                nc.vector.tensor_scalar(idx[:, k % 2:k % 2 + 1], gidx[:, bass.ds(col, 1)], float(split), float(cb), ALU.mult, ALU.add).then_inc(idx_ready, 1)

            def unpack(i, last, k):
                name, cb, t, rows = dequant_blocks(i, last)[k]
                width = NB if name != "down" else D
                n = i * BLOCKS_PER_PAIR + (k + 1)
                transfers = i * (16 * ((BLOCKS_PER_PAIR + 1 - k % 2) // 2)) + 16 * (k // 2 + 1)
                dve.wait_ge(q_in[k % 2], transfers)
                q = dq_q[0:rows, k % 2, 0:width]
                nc.vector.tensor_scalar(q, q, shift_row[0:rows, 0:1], PACK * 2 - 1, ALU.logical_shift_right,
                                        ALU.bitwise_and).then_inc(dq_chain, 1)
                dve.wait_ge(gathered[k % 2], transfers)
                dve.wait_ge(dq_chain, n)
                nc.vector.scalar_tensor_tensor(out=q.bitcast(F32), in0=q, scalar=1.0,
                                               in1=dq_t[0:rows, k % 2, width:2 * width].bitcast(I32), op0=ALU.subtract,
                                               op1=ALU.subtract).then_inc(unpacked, 1)

            def x_low(m):
                cols = slice(m * P, (m + 1) * P)
                dve.wait_ge(xt_high, m + 1)
                nc.vector.tensor_tensor(x2T[:, LOW, :, cols], x_bank(m).rearrange("p (c n) -> p c n", c=DC),
                                        x2T[:, HIGH, :, cols].bitcast(F32), ALU.subtract).then_inc(xt_low, 1)

            def ffn_norm(k, rows):
                for m in range(2):
                    nc.vector.bn_stats(bn[:, 2 * k + m], rows[:, m]).then_inc(f_stat, 1)
                dve.wait_ge(f_stat, 2 * k + 2)
                for m in range(2):
                    nc.vector.bn_aggr(mv[:, 2 * k + m], bn[:, 2 * k + m]).then_inc(f_mv, 1)
                dve.wait_ge(f_mv, 2 * k + 2)
                nc.vector.tensor_scalar(veps[:, 2 * k:2 * k + 2], mv[:, 2 * k:2 * k + 2, 1], EPS, None, ALU.add).then_inc(f_var, 1)

            def ffn_norm_apply(k, rows, dst):
                dve.wait_ge(f_rstd, k + 1)
                for m in range(2):
                    op = nc.vector.tensor_scalar(dst[:, m], rows[:, m], mv[:, 2 * k + m, 0:1], rstd[:, 2 * k + m:2 * k + m + 1],
                                                 ALU.subtract, ALU.mult)
                op.then_inc(f_ln, 1)

            def split_gu(n):
                w = P if n < NT - 1 else LAST_N
                dve.wait_ge(gu_high, n + 1)
                nc.vector.tensor_tensor(wgu[:, n, LOW, :, :, 0:w], st_gu[:, n % 2, :, :, 0:w],
                                        wgu[:, n, HIGH, :, :, 0:w].bitcast(F32), ALU.subtract).then_inc(gu_low, 1)

            def follow(i, last, steps):
                ring = Ring(i, steps)
                blocks = len(dequant_blocks(i, last))

                def evacuate(job):
                    done, bank = ring.high(job), ring.bank(job)
                    if job[0] == "K":
                        j = int(job[1])

                        def dst(part):
                            return [kT[0:HD, part, j].rearrange("p (b t s) -> p t b s", b=2, t=2),
                                    k3T[TAIL * j:TAIL * (j + 1), part].rearrange("p (b t s) -> p t b s", b=2, t=2)]

                        low(done, bank, dst(LOW), dst(HIGH), shape=(("p (t b s) -> p t b s",), {"b": 2, "t": 2}))
                    elif job[0] == "V":
                        low(done, bank, v_sb[:, LOW, int(job[1])], v_sb[:, HIGH, int(job[1])], KV * HD)
                    elif job[0] == "Q":
                        q, j = int(job[1]) % 2, int(job[3])

                        def dst(part):
                            return [qT[q][0:HD, part, j], q3T[q][TAIL * j:TAIL * (j + 1), part]]

                        low(done, bank, dst(LOW), dst(HIGH), 2 * TOK, scale=SCALE)
                    elif job[0] == "o":
                        kv, j = int(job[1:]) // QT, int(job[1:]) % QT
                        low(done, bank, woT[kv % 2][:, LOW, j], woT[kv % 2][:, HIGH, j])
                    elif job[0] in "kvq":
                        dst, t = {"k": wkT, "v": wvT, "q": wqT}[job[0]], int(job[1:])
                        cols = slice(t * P, (t + 1) * P)
                        low(done, bank, dst[:, LOW, :, cols], dst[:, HIGH, :, cols], shape=by_chunk)
                    else:
                        low(done, bank, hT[:, LOW, :, int(job[1]), :], hT[:, HIGH, :, int(job[1]), :], shape=by_chunk)

                def maxima(u):
                    dve.wait_ge(s_full, i * UNITS + (u + 1))
                    nc.vector.tensor_reduce(negmax[:, u % 2], ps_scores[:, u % 2].rearrange("p (h s) -> p h s", h=GROUP),
                                            AX.X, ALU.max, negate=True).then_inc(maxed, 1)

                def reciprocals(u):
                    dve.wait_ge(expd, i * UNITS + (u + 1))
                    nc.vector.reciprocal(rsums[:, u % 2], sums[:, u % 2]).then_inc(recip, 1)

                def attention_out(u):
                    b = u % 2
                    dve.wait_ge(ring_high, ring.high(f"O{u}"))
                    o = ps_ring[0:HD, ring.bank(f"O{u}")].rearrange("p (h q) -> p h q", h=GROUP)
                    hi, lo = oT[:, b, HIGH].bitcast(F32), oT[:, b, LOW]
                    for j in range(QT):
                        nc.vector.tensor_tensor(lo[HD:P, j], o[TAIL * j:TAIL * (j + 1), GROUP - 1], hi[HD:P, j], ALU.subtract)
                    nc.vector.tensor_tensor(lo[0:HD], o[:, 0:QT], hi[0:HD], ALU.subtract).then_inc(ring_free, 1)

                def add_projection(u):
                    b = u % 2
                    if u < 2:
                        dve.wait_ge(xres_in, i * 16 + 16)
                    else:
                        dve.wait_ge(ring_free, ring.done(f"Y{u - 2}"))
                    dve.wait_ge(ring_full, ring.done(f"Y{u}"))
                    nc.vector.scalar_tensor_tensor(out=xres[:, b], in0=ps_ring[:, ring.bank(f"Y{u}")], scalar=tgate[:, 0:1],
                                                   in1=xres[:, b], op0=ALU.mult, op1=ALU.add).then_inc(ring_free, 1)

                for step in steps:
                    n = int(step[1]) if step[1:] else 0
                    if step in ring.split and step[0] != "O":
                        evacuate(step)
                    elif step[0] == "S":
                        maxima(n)
                    elif step[0] == "R":
                        reciprocals(n)
                    elif step[0] == "P":
                        for t in range(2):
                            dve.wait_ge(pt_high, i * (2 * UNITS) + (2 * n + t + 1))
                            nc.vector.tensor_tensor(pT[:, LOW, t], ps_pt[:, t], pT[:, HIGH, t].bitcast(F32), ALU.subtract).then_inc(pt_low, 1)
                    elif step[0] == "O":
                        attention_out(n)
                    elif step == "Z":
                        small_work()
                    elif step[0] == "Y":
                        add_projection(n)
                    elif step[0] == "D" and n < blocks:
                        unpack(i, last, n)
                        if n + 2 < blocks:
                            indices(i, last, n + 2)
                    elif step == "L":
                        layer_norm(i + 1, i * 16 + 32)
                    elif step == "A":
                        layer_norm_apply(i + 1)
                    elif step[0] == "N":
                        dve.wait_ge(x1_in[n], 16)
                        ffn_norm(n, x1n[:, 2 * n:2 * n + 2])
                    elif step[0] == "T":
                        ffn_norm_apply(n, x1n[:, 2 * n:2 * n + 2], x1n[:, 2 * n:2 * n + 2])
                    elif step[0] == "W":
                        split_gu(n)
                    elif step[0] == "X":
                        x_low(n)

            def body(i, last):
                indices(i, last, 0)
                indices(i, last, 1)
                follow(i, last, pair_steps(last))

            follow(-1, False, PRO_STEPS)
            with dve.Fori(0, PAIRS - 1, 1) as i:
                body(i, False)
            body(PAIRS - 1, True)

            dve.wait_ge(ring_free, ATT_JOBS)
            ffn_norm(BATCH // 2 - 1, xres)
            ffn_norm_apply(BATCH // 2 - 1, xres, x1n)

            def split_d(n):
                w = P if n < NT - 1 else LAST_N
                dve.wait_ge(d_high, n + 1)
                nc.vector.tensor_tensor(wd[0:w, n, LOW], st_d[0:w, n % 2], wd[0:w, n, HIGH].bitcast(F32),
                                        ALU.subtract).then_inc(d_low, 1)

            for hf in range(2):
                for n in range(NT):
                    w, at = (P if n < NT - 1 else LAST_N), hf * NT + n
                    dve.wait_ge(silu_done, at + 1)
                    dve.wait_ge(u_full, at + 1)
                    nc.vector.tensor_tensor(silu[0:w, at % 2], ps_scores[0:w, at % 2, 512:1024], silu[0:w, at % 2], ALU.mult).then_inc(h_done, 1)
                    if hf == 0:
                        if n == 1:
                            for m in range(EARLY, BATCH):
                                x_low(m)
                        split_d(n)
                    dve.wait_ge(h_high, at + 1)
                    nc.vector.tensor_tensor(hidden[0:w, at % 2, LOW], silu[0:w, at % 2],
                                            hidden[0:w, at % 2, HIGH].bitcast(F32), ALU.subtract).then_inc(h_low, 1)
                    if hf == 0 and n + W_EARLY < NT:
                        split_gu(n + W_EARLY)
                dve.wait_ge(res_in, 16 * (hf + 1))
                for m in range(4):
                    dve.wait_ge(f_y_full, hf * 4 + m + 1)
                    bank = ps_pt[:, m] if m < 2 else ps_ring[:, m - 2]
                    nc.vector.scalar_tensor_tensor(out=res[:, m], in0=bank, scalar=tgate[:, 1:2], in1=res[:, m],
                                                   op0=ALU.mult, op1=ALU.add).then_inc(f_y_free, 1)

        @block.tensor
        def _(pe):
            pe.wait_ge(const_ready, 2)
            for _ in range(WARM_UP):
                nc.tensor.transpose(ps_scores[:, 1, 0:P], ident[:], ident[:])

            def transpose_x(m):
                pe.wait_ge(f_ln, m // 2 + 1)
                if m in (2, 3):
                    pe.wait_ge(xt_low, m - 1)
                if m >= EARLY:
                    pe.wait_ge(h_done, 1)
                for c in range(DC):
                    op = nc.tensor.transpose(x_bank(m)[:, c * P:(c + 1) * P], x1n[:, m % EARLY, c * P:(c + 1) * P], ident[:])
                op.then_inc(xt_full, 1)

            def gate_or_up(hf, n, mat):
                w, at = (P if n < NT - 1 else LAST_N), hf * NT + n
                if hf == 0:
                    pe.wait_ge(gu_low, n + 1)
                if at < 3:
                    pe.wait_ge(xt_low, (4, 6, 8)[at])
                if at >= 2:
                    pe.wait_ge(silu_done if mat == 0 else h_done, at - 1)
                for c in range(DC):
                    for k, (a, b) in enumerate(PASSES):
                        op = nc.tensor.matmul(ps_scores[0:w, at % 2, mat * 512:mat * 512 + 512], wgu[:, n, a, mat, c, 0:w],
                                              x2T[:, b, c, hf * 512:(hf + 1) * 512],
                                              start=(c == 0 and k == 0), stop=(c == DC - 1 and k == len(PASSES) - 1))
                op.then_inc(g_full if mat == 0 else u_full, 1)

            def follow(i, steps):
                ring = Ring(i, steps)

                def open_slot(job):
                    if not (ring.prologue and ring.slot(job) == 0):
                        pe.wait_ge(ring_free, ring.slot(job))
                    return ring_bank(ring.bank(job))

                def product(dst, stationary, moving):
                    for c in range(DC):
                        for n, (a, b) in enumerate(PASSES):
                            op = nc.tensor.matmul(dst, stationary(a, c), moving(b, c), start=(c == 0 and n == 0),
                                                  stop=(c == DC - 1 and n == len(PASSES) - 1))
                    return op

                def project(job):
                    bank = open_slot(job)
                    needs = ["H0", "H1", "H2", "H3"] if job[0] == "K" or job[:2] in ("Q0", "Q1") else []
                    if steps is PRO_STEPS and job[0] == "K":
                        needs.append(f"k{job[1]}")
                    if steps is PRO_STEPS and job[0] == "Q":
                        needs.append(f"q{int(job[1]) * QT + int(job[3])}")
                    if needs:
                        pe.wait_ge(ring_free, ring.done(max(needs, key=ring.jobs.index)))
                    if job[0] == "K":
                        cols = slice(int(job[1]) * P, (int(job[1]) + 1) * P)
                        op = product(bank, lambda a, c: wkT[:, a, c, cols], lambda b, c: hT[:, b, c])
                    elif job[0] == "V":
                        m = int(job[1])
                        op = product(bank[:, 0:KV * HD], lambda a, c: hT[:, a, c, m], lambda b, c: wvT[:, b, c])
                    elif job[0] == "Q":
                        t = int(job[1]) * QT + int(job[3])
                        op = product(bank[:, 0:2 * TOK], lambda a, c: wqT[:, a, c, t * P:(t + 1) * P],
                                     lambda b, c: hT[:, b, c, 0:2])
                    elif job[0] in "kvq":
                        t = int(job[1:])
                        raw, arrived, count = {"k": (wk_raw, wk_in, 32), "v": (wv_raw, wv_in, 16), "q": (wq_raw, wq_in[t // QT % KV], 32)}[job[0]]
                        pe.wait_ge(arrived, count)
                        for c in range(DC):
                            op = nc.tensor.transpose(bank[:, c * P:(c + 1) * P], raw[:, t, c * P:(c + 1) * P], ident[:])
                    elif job[0] == "o":
                        kv, j = int(job[1:]) // QT, int(job[1:]) % QT
                        pe.wait_ge(wo_in, 16)
                        for b in range(DC):
                            at = (kv * GROUP + QT) * HD + j * TAIL - HD
                            nc.tensor.transpose(bank[:, b * P:(b + 1) * P], wo_raw[:, b, at:at + P], ident[:])
                            at = (kv * GROUP + j) * HD
                            op = nc.tensor.transpose(bank[0:HD, b * P:(b + 1) * P], wo_raw[:, b, at:at + HD], ident[:])
                    else:
                        m = int(job[1])
                        if m < 2:
                            pe.wait_ge(ln_done, i + 2)
                        else:
                            pe.wait_ge(ctx_in, i * 16 + 32)
                        for c in range(DC):
                            op = nc.tensor.transpose(bank[:, c * P:(c + 1) * P], xin[:, m, c * P:(c + 1) * P], ident[:])
                    op.then_inc(ring_full, 1)

                def scores(u):
                    kv, b = u // 2 % KV, u % 2
                    if u == UNITS:
                        pe.wait_ge(ring_free, ring.done("K2"))
                    elif u == 2:
                        pe.wait_ge(ring_free, ring.first)
                    elif b == 0:
                        pe.wait_ge(ring_free, ring.done(f"Q{kv}.2"))
                    q = slice(b * TOK, (b + 1) * TOK)
                    s = slice(b * 256, (b + 1) * 256)
                    for h in range(GROUP):
                        for n, (pa, pb) in enumerate(PASSES):
                            stat = qT[kv % 2][0:HD, pa, h, q] if h < QT else q3T[kv % 2][0:HD, pa, q]
                            mov = kT[0:HD, pb, kv, s] if kv < QT else k3T[0:HD, pb, s]
                            op = nc.tensor.matmul(ps_scores[:, b, h * 256:(h + 1) * 256], stat, mov, start=(n == 0),
                                                  stop=(n == len(PASSES) - 1), skip_group_check=True)
                    op.then_inc(s_full, 1)

                def transpose_probs(u):
                    pe.wait_ge(normed, i * UNITS + (u + 1))
                    for t in range(2):
                        for h in range(GROUP):
                            op = nc.tensor.transpose(ps_pt[:, t, h * P:(h + 1) * P], probs[:, u % 2, h, t * P:(t + 1) * P], ident[:])
                        op.then_inc(pt_full, 1)

                def attend(u):
                    kv, b = u // 2, u % 2
                    bank = open_slot(f"O{u}")
                    if u == 0:
                        pe.wait_ge(ring_free, ring.done("V3"))
                    for t in range(2):
                        pe.wait_ge(pt_low, i * (2 * UNITS) + (2 * u + t + 1))
                        block_ = b if t == 0 else 2 + b
                        for n, (pa, pb) in enumerate(PASSES):
                            op = nc.tensor.matmul(bank[0:HD], v_sb[:, pa, block_, kv * HD:(kv + 1) * HD], pT[:, pb, t],
                                                  start=(t == 0 and n == 0), stop=(t == 1 and n == len(PASSES) - 1))
                    op.then_inc(ring_full, 1)

                def project_out(u):
                    bank = open_slot(f"Y{u}")
                    pe.wait_ge(ring_free, ring.done(f"O{u}"))
                    if u % 2 == 0:
                        kv = u // 2
                        pe.wait_ge(wo_there[kv % 2], i * 32 + (16, 32, 32, 48)[kv])
                    for j in range(QT):
                        for n, (pa, pb) in enumerate(PASSES):
                            op = nc.tensor.matmul(bank, oT[:, u % 2, pa, j], woT[u // 2 % 2][:, pb, j],
                                                  start=(j == 0 and n == 0), stop=(j == QT - 1 and n == len(PASSES) - 1))
                    op.then_inc(ring_full, 1)

                for step in steps:
                    if step in ring.split and step[0] != "O":
                        project(step)
                    elif step in ("G", "U"):
                        gate_or_up(0, 0, int(step == "U"))
                    elif step[0] == "X":
                        transpose_x(int(step[1]))
                    elif step[0] in "SPOY":
                        {"S": scores, "P": transpose_probs, "O": attend, "Y": project_out}[step[0]](int(step[1]))

            def body(i, last):
                follow(i, pair_steps(last))

            follow(-1, PRO_STEPS)
            with pe.Fori(0, PAIRS - 1, 1) as i:
                body(i, False)
            body(PAIRS - 1, True)

            def down_tile(hf, n):
                w, at = (P if n < NT - 1 else LAST_N), hf * NT + n
                pe.wait_ge(h_low, at + 1)
                if hf == 0:
                    pe.wait_ge(d_low, n + 1)
                if n == 0:
                    if hf == 0:
                        pe.wait_ge(ring_free, ATT_JOBS)
                    else:
                        pe.wait_ge(f_y_free, 4)
                for m in range(4):
                    bank = ps_pt[:, m] if m < 2 else ps_ring[:, m - 2]
                    for k, (a, b) in enumerate(PASSES):
                        op = nc.tensor.matmul(bank, hidden[0:w, at % 2, a, m * P:(m + 1) * P], wd[0:w, n, b],
                                              start=(n == 0 and k == 0), stop=(n == NT - 1 and k == len(PASSES) - 1))
                    if n == NT - 1:
                        op.then_inc(f_y_full, 1)
                if n < NT - 1:
                    op.then_inc(down_done, 1)

            for hf in range(2):
                tokens = slice(hf * 512, (hf + 1) * 512)
                for n in range(NT):
                    w, at = (P if n < NT - 1 else LAST_N), hf * NT + n
                    if at > 0:
                        gate_or_up(hf, n, 0)
                        gate_or_up(hf, n, 1)
                    if at == 1:
                        for m in range(EARLY, BATCH):
                            transpose_x(m)
                    if at > 0:
                        down_tile((at - 1) // NT, (at - 1) % NT)
            down_tile(1, NT - 1)


_INS = ["x", "ctx_4096", "g_xattn", "g_ffn", "L0_xattn_Wq", "L0_xattn_Wk", "L0_xattn_Wv", "L0_xattn_Wo"] + [
    f"L0_ffn_{m}_{w}" for m in ("gate", "up", "down") for w in ("qweight", "scales", "qzeros", "g_idx")]


def kernel(**inputs):
    import numpy as _np
    import concourse.bacc as _bacc
    from concourse import mybir as _mybir
    from concourse.bass_utils import run_bass_kernel_spmd as _run

    nc = _bacc.Bacc("TRN2", target_bir_lowering=False, num_devices=1)
    arrays, args = {}, []
    for name in _INS:
        a = _np.ascontiguousarray(inputs[name])
        arrays[f"in_{name}_dram"] = a
        args.append(nc.dram_tensor(f"in_{name}_dram", a.shape, _mybir.dt.from_np(a.dtype), kind="ExternalInput").ap())
    out = nc.dram_tensor("out_0_dram", (BATCH, TOK, D), F32, kind="ExternalOutput").ap()
    build(nc, *args[:8], args[8:12], args[12:16], args[16:20], out)
    r = _run(nc, [arrays], core_ids=[0])
    return r.results[0]["out_0_dram"]
```
